# Optimizing a Trainium2 kernel written in Bass

```python
import numpy as np
import jax
import jax.numpy as jnp

def _softmax(x, axis=-1):
    return jax.nn.softmax(x, axis=axis)

def _gelu(x):
    return jax.nn.gelu(x, approximate=True)

def _silu(x):
    return jax.nn.silu(x)

def _sigmoid(x):
    return jax.nn.sigmoid(x)

def _layernorm(x, axis=-1, eps=1e-05):
    m = jnp.mean(x, axis=axis, keepdims=True)
    v = jnp.var(x, axis=axis, keepdims=True)
    return (x - m) / jnp.sqrt(v + eps)

def _scatter_add(tgt, idx, src, axis=0):
    return tgt.at[idx].add(src)

def _segment_sum(src, seg, n):
    return jax.ops.segment_sum(src, seg, n)
kernel_name = 'mk_adaln_d1_jaxref_r8_63fd71'

def setup_inputs(seed: int=0):
    np.random.seed(seed)
    _w = jnp.asarray

    def _L0_attn_setup():
        import jax, jax.numpy as jnp
        import numpy as np
        B, T, D = (4, 256, 128)
        H, DK, DV = (8, 128, 128)

        def _l2norm(u, eps=1e-12):
            n = jnp.sqrt(jnp.sum(u * u, axis=-1, keepdims=True))
            return u / jnp.maximum(n, eps)
        key = jax.random.key(seed)
        ks = jax.random.split(key, 6)
        s = 0.02
        x = jax.random.normal(ks[0], (B, T, D), dtype=jnp.float32)
        Wq = jax.random.normal(ks[1], (D, H * DK), dtype=jnp.float32) * s
        Wk = jax.random.normal(ks[2], (D, H * DK), dtype=jnp.float32) * s
        Wv = jax.random.normal(ks[3], (D, H * DV), dtype=jnp.float32) * s
        Wg = jax.random.normal(ks[4], (D, H * DK), dtype=jnp.float32) * s
        Wo = jax.random.normal(ks[5], (H * DV, D), dtype=jnp.float32) * s
        return {'x': x, 'Wq': Wq, 'Wk': Wk, 'Wv': Wv, 'Wg': Wg, 'Wo': Wo}
    _L0_attn_in = _L0_attn_setup()

    def _L0_ffn_setup():
        import jax, jax.numpy as jnp
        import numpy as np
        B, T, D, H, E = (4, 256, 128, 512, 8)
        key = jax.random.key(seed)
        ks = jax.random.split(key, 7)
        x = jax.random.normal(ks[0], (B, T, D), dtype=jnp.float32)
        Wg = jax.random.normal(ks[1], (D, E), dtype=jnp.float32) / np.sqrt(D)
        bg = jax.random.normal(ks[2], (E,), dtype=jnp.float32) * 0.01
        W1 = jax.random.normal(ks[3], (E, D, H), dtype=jnp.float32) / np.sqrt(D)
        b1 = jax.random.normal(ks[4], (E, H), dtype=jnp.float32) * 0.01
        W2 = jax.random.normal(ks[5], (E, H, D), dtype=jnp.float32) / np.sqrt(H)
        b2 = jax.random.normal(ks[6], (E, D), dtype=jnp.float32) * 0.01
        return {'x': x, 'Wg': Wg, 'bg': bg, 'W1': W1, 'b1': b1, 'W2': W2, 'b2': b2}
    _L0_ffn_in = _L0_ffn_setup()
    _L0_c = _w((lambda *s: np.random.randn(*s).astype(np.float32) * 0.05)(8, 128))
    _L0_wmod = _w((lambda *s: np.random.randn(*s).astype(np.float32) * 0.05)(128, 6 * 128) * 128 ** (-0.5))
    _d = {'L0_attn_x': _L0_attn_in['x'], 'L0_attn_Wq': _L0_attn_in['Wq'], 'L0_attn_Wk': _L0_attn_in['Wk'], 'L0_attn_Wv': _L0_attn_in['Wv'], 'L0_attn_Wg': _L0_attn_in['Wg'], 'L0_attn_Wo': _L0_attn_in['Wo'], 'L0_ffn_Wg': _L0_ffn_in['Wg'], 'L0_ffn_bg': _L0_ffn_in['bg'], 'L0_ffn_W1': _L0_ffn_in['W1'], 'L0_ffn_b1': _L0_ffn_in['b1'], 'L0_ffn_W2': _L0_ffn_in['W2'], 'L0_ffn_b2': _L0_ffn_in['b2'], 'L0_c': _L0_c, 'L0_wmod': _L0_wmod}
    _x0 = _d['L0_attn_x']
    _d['L0_attn_x'] = jax.random.normal(jax.random.fold_in(jax.random.key(seed), 1), (8, 1024, 128), dtype=_x0.dtype)
    del _x0
    return _d

def reference(L0_attn_x, L0_attn_Wq, L0_attn_Wk, L0_attn_Wv, L0_attn_Wg, L0_attn_Wo, L0_ffn_Wg, L0_ffn_bg, L0_ffn_W1, L0_ffn_b1, L0_ffn_W2, L0_ffn_b2, L0_c, L0_wmod):

    def _L0_attn_ref(x, Wq, Wk, Wv, Wg, Wo):
        import jax, jax.numpy as jnp
        import numpy as np
        B, T, D = (4, 256, 128)
        H, DK, DV = (8, 128, 128)

        def _l2norm(u, eps=1e-12):
            n = jnp.sqrt(jnp.sum(u * u, axis=-1, keepdims=True))
            return u / jnp.maximum(n, eps)
        Bb, Tt, _ = x.shape
        q = _l2norm((x @ Wq).reshape(Bb, Tt, H, DK))
        k = _l2norm((x @ Wk).reshape(Bb, Tt, H, DK))
        v = (x @ Wv).reshape(Bb, Tt, H, DV)
        alpha = jax.nn.sigmoid(x @ Wg).reshape(Bb, Tt, H, DK)

        def step(S, qkva):
            q_t, k_t, v_t, a_t = qkva
            S = a_t[..., None] * S + k_t[..., None] * v_t[:, :, None, :]
            o_t = jnp.einsum('bhkv,bhk->bhv', S, q_t)
            return (S, o_t)
        S0 = jnp.zeros((Bb, H, DK, DV), dtype=x.dtype)
        xs = (q.swapaxes(0, 1), k.swapaxes(0, 1), v.swapaxes(0, 1), alpha.swapaxes(0, 1))
        _, o = jax.lax.scan(step, S0, xs)
        o = o.swapaxes(0, 1).reshape(Bb, Tt, H * DV)
        return o @ Wo

    def _L0_ffn_ref(x, Wg, bg, W1, b1, W2, b2):
        import jax, jax.numpy as jnp
        import numpy as np
        B, T, D, H, E = (4, 256, 128, 512, 8)
        gate_scores = x @ Wg + bg
        top1 = jnp.argmax(gate_scores, axis=-1)
        onehot = jax.nn.one_hot(top1, Wg.shape[-1], dtype=x.dtype)
        h = jax.nn.relu(jnp.einsum('btd,edh->beth', x, W1) + b1[None, :, None, :])
        y = jnp.einsum('beth,ehd->betd', h, W2) + b2[None, :, None, :]
        out = jnp.einsum('betd,bte->btd', y, onehot)
        return out
    x = L0_attn_x
    mod = (_silu(L0_c) @ L0_wmod).reshape(L0_c.shape[0], 6, 1, -1)
    sa, ca, ga, sb, cb, gb = (mod[:, 0], mod[:, 1], mod[:, 2], mod[:, 3], mod[:, 4], mod[:, 5])
    ga = (2 * (ga >= 0) - 1) * jnp.maximum(jnp.abs(ga), 0.25)
    gb = (2 * (gb >= 0) - 1) * jnp.maximum(jnp.abs(gb), 0.25)
    h = _layernorm(x, axis=-1) * (1 + ca) + sa
    x = x + ga * _L0_attn_ref(h, L0_attn_Wq, L0_attn_Wk, L0_attn_Wv, L0_attn_Wg, L0_attn_Wo)
    h = _layernorm(x, axis=-1) * (1 + cb) + sb
    x = x + gb * _L0_ffn_ref(h, L0_ffn_Wg, L0_ffn_bg, L0_ffn_W1, L0_ffn_b1, L0_ffn_W2, L0_ffn_b2)
    return x

_drawn_inputs = setup_inputs


def setup_inputs(seed=0):
    import zlib

    import numpy as np

    out = dict(_drawn_inputs(seed))
    spreads = {}
    factors = {'L0_attn_Wq': 5.133,
     'L0_attn_Wk': 5.41,
     'L0_attn_Wv': 5.507,
     'L0_attn_Wg': 8.0,
     'L0_attn_Wo': 5.847,
     'L0_ffn_bg': 3.695,
     'L0_ffn_b1': 32.798,
     'L0_ffn_b2': 22.485}
    for name, (base, spread) in spreads.items():
        noise = np.random.default_rng([zlib.crc32(name.encode()), seed]).standard_normal(out[name].shape)
        drawn = base * np.exp(spread * noise) if base else spread * noise
        out[name] = jnp.asarray(drawn.astype(out[name].dtype))
    for name, factor in factors.items():
        out[name] = (out[name] * factor).astype(out[name].dtype)
    return out
```

```python
from contextlib import ExitStack

import concourse.bass as bass
from concourse import mybir

F32 = mybir.dt.float32
I32 = mybir.dt.int32
ALU = mybir.AluOpType
ACT = mybir.ActivationFunctionType
AX = mybir.AxisListType.X

P = 128
B, T, D = 8, 1024, 128
H = 8
E, F = 8, 512
FC = F // P
NCHUNK = B * T // P
LEVELS = [0, 1, 2, 4, 8, 16, 32, 64]
NL = len(LEVELS)
G = 2
HG = H // G
W = HG * P
LN_EPS = 1e-5
NORM_EPS = 1e-12
GATE_FLOOR = 0.25
SA, CA, GA, SB, CB, GB = range(6)
T_AT = {}
for _m in (2, 4, 8, 16, 32, 64, 128):
    T_AT[_m] = sum(H * P // n for n in T_AT)
T_LEN = sum(H * P // n for n in T_AT)


def adaln_gla_moe(nc, x, wq, wk, wv, wg, wo, gate_w, gate_b, w1, b1, w2, b2, c, wmod,
                  ident, level_masks, diag_mask, descending, out):
    with ExitStack() as ctx:
        def sb(name, shape, dt=F32):
            return ctx.enter_context(nc.sbuf_tensor(name, shape, dt))

        def bank(name):
            return ctx.enter_context(nc.psum_tensor(name, [P, 512], F32))

        def sem(name):
            return ctx.enter_context(nc.semaphore(name))

        wq_sb, wk_sb, wv_sb, wg_sb = (sb(f"w{n}_sb", [P, H * P]) for n in "qkvg")
        wo_sb = sb("wo_sb", [P, H, D])
        w1_sb = sb("w1_sb", [P, E, F])
        w2_sb = sb("w2_sb", [P, E, FC, D])
        b1_sb = sb("b1_sb", [P, E * FC])
        b2_sb = sb("b2_sb", [E, D])
        gate_w_sb = sb("gate_w_sb", [P, E])
        gate_b_sb = sb("gate_b_sb", [P, E])
        ident_sb = sb("ident_sb", [P, P])
        masks_sb = sb("masks_sb", [P, NL - 1, W // 2], I32)
        diag_sb = sb("diag_sb", [P, W], I32)
        desc_sb = sb("desc_sb", [P, E])
        ones_col = sb("ones_col", [P, 1])
        minus_half = sb("minus_half", [P, 2 * H])
        c_sb = sb("c_sb", [B, P])
        silu_c = sb("silu_c", [B, P])
        c_t = sb("c_t", [P, B])
        c_wide = sb("c_wide", [P, B, P])
        wmod_sb = sb("wmod_sb", [P, 6, D])
        mod_t = sb("mod_t", [P, 6, B])
        gates = sb("gates", [P, 2, B, D])
        gate_sign = sb("gate_sign", [P, B, D])
        state = sb("state", [P, B * H * P])
        x_next = sb("x_next", [P, D])
        x_res = sb("x_res", [P, D])
        stats = sb("stats", [P, 2, 6])
        mean_var = sb("mean_var", [P, 2, 2])
        var_eps = sb("var_eps", [P, 2])
        rstd = sb("rstd", [P, 2])
        xn = sb("xn", [P, D])
        xn2 = sb("xn2", [P, D])
        h_t = sb("h_t", [P, P])
        h2_t = sb("h2_t", [P, P])
        alpha = sb("alpha", [P, H * P])
        q_raw = sb("q_raw", [P, H * P])
        q_sq = sb("q_sq", [P, H * P])
        k_sq = sb("k_sq", [P, H * P])
        qd = sb("qd", [P, H * P])
        kd = sb("kd", [P, H * P])
        t_prod = sb("t_prod", [P, T_LEN])
        scores = sb("scores", [P, H * P])
        v_sb = sb("v_sb", [P, H * P])
        k_tok = sb("k_tok", [P, H * P])
        o_sb = sb("o_sb", [P, H * P])
        o_t = sb("o_t", [P, H * P])
        sumsq = sb("sumsq", [P, 2 * H])
        rnorm = sb("rnorm", [P, 2 * H])
        y_gated = sb("y_gated", [P, D])
        x1 = sb("x1", [P, D])
        gate_s = sb("gate_s", [P, E])
        gate_max = sb("gate_max", [P, 1])
        gate_rank = sb("gate_rank", [P, E])
        gate_first = sb("gate_first", [P, 1])
        onehot = sb("onehot", [P, E])
        onehot_t = sb("onehot_t", [E, P])
        hid = sb("hid", [P, 2, FC, P])
        acc = sb("acc", [P, 2, D])
        ffn_gated = sb("ffn_gated", [P, D])
        out_sb = sb("out_sb", [P, D])

        bank_a = bank("bank_a")
        bank_k = bank("bank_k")
        bank_q = bank("bank_q")
        bank_l = [bank("bank_l0"), bank("bank_l1")]
        bank_m = bank("bank_m")
        bank_h = bank("bank_h")
        bank_y = bank("bank_y")

        weights_in = sem("weights_in")
        x_next_in = sem("x_next_in")
        x_res_in = sem("x_res_in")
        out_free = sem("out_free")
        setup_dve = sem("setup_dve")
        setup_pe = sem("setup_pe")
        setup_act = sem("setup_act")
        setup_pool = sem("setup_pool")
        a_done, k_done, q_done, v_done = (sem(f"{n}_done") for n in "akqv")
        norms_done = sem("norms_done")
        level_done = sem("level_done")
        k_tok_done = sem("k_tok_done")
        o_done = sem("o_done")
        update_done = sem("update_done")
        o_t_done = sem("o_t_done")
        y_done = sem("y_done")
        xn_t_done = sem("xn_t_done")
        xn2_t_done = sem("xn2_t_done")
        gate_done = sem("gate_done")
        onehot_t_done = sem("onehot_t_done")
        bias_done = sem("bias_done")
        hid_done = sem("hid_done")
        expert_done = sem("expert_done")
        alpha_ready = sem("alpha_ready")
        kd_first = sem("kd_first")
        k_sq_ready = sem("k_sq_ready")
        q_raw_ready = sem("q_raw_ready")
        q_sq_ready = sem("q_sq_ready")
        v_ready = sem("v_ready")
        k_tok_ready = sem("k_tok_ready")
        o_t_ready = sem("o_t_ready")
        hid_ready = sem("hid_ready")
        qd_ready = sem("qd_ready")
        kd_ready = sem("kd_ready")
        t_ready = sem("t_ready")
        scores_ready = sem("scores_ready")
        sumsq_ready = sem("sumsq_ready")
        rnorm_ready = sem("rnorm_ready")
        var_ready = sem("var_ready")
        rstd_ready = sem("rstd_ready")
        xn_ready = sem("xn_ready")
        xn2_ready = sem("xn2_ready")
        h_t_ready = sem("h_t_ready")
        h2_t_ready = sem("h2_t_ready")
        onehot_ready = sem("onehot_ready")
        onehot_t_ready = sem("onehot_t_ready")
        acc_ready = sem("acc_ready")
        o_ready = sem("o_ready")
        state_ready = sem("state_ready")
        x1_ready = sem("x1_ready")
        out_ready = sem("out_ready")
        dve_step = sem("dve_step")

        NU = NL
        NW = 19

        def x_rows(tensor, i):
            return tensor[bass.ds(i % B, 1), bass.ds((i // B) * P, P), :].rearrange("a t d -> (a t) d")

        def cols(g):
            return slice(g * W, (g + 1) * W)

        def head(buf, h):
            return buf[:, h * P:(h + 1) * P]

        def halves(buf, g, m):
            return buf[:, cols(g)].rearrange("p (n two m) -> p n two m", two=2, m=m)

        def block_products(g, m, side):
            n = W // m
            buf = alpha[:, cols(g)] if m == 1 else t_prod[:, T_AT[m] + g * n:T_AT[m] + (g + 1) * n]
            return buf.rearrange("p (n two) -> p n two", two=2)[:, :, side]

        def later(i):
            return not (isinstance(i, int) and i == 0)

        def spread(ap, m):
            return ap.unsqueeze(2).broadcast_to((P, ap.shape[1], m))

        block = ctx.enter_context(nc.Block())

        @block.sync
        def _(sp):
            loads = [(c_sb[:, :], c), (wmod_sb[:, :, :].rearrange("p a b -> p (a b)"), wmod),
                     (ident_sb[:, :], ident), (wg_sb[:, :], wg), (wk_sb[:, :], wk), (wq_sb[:, :], wq),
                     (wv_sb[:, :], wv), (masks_sb[:, :, :].rearrange("p a b -> p (a b)"), level_masks),
                     (diag_sb[:, :], diag_mask), (wo_sb[:, :, :], wo), (gate_w_sb[:, :], gate_w),
                     (gate_b_sb[:, :], gate_b), (desc_sb[:, :], descending), (b1_sb[:, :], b1),
                     (b2_sb[:, :], b2)]
            sp.dma_start(x_next[:, :], x_rows(x, 0)).then_inc(x_next_in, 16)
            sp.dma_start(x_res[:, :], x_rows(x, 0)).then_inc(x_res_in, 16)
            for to, of in loads:
                sp.dma_start(to, of).then_inc(weights_in, 16)
            for e in range(0, E, 4):
                sp.dma_start(w1_sb[:, e:e + 4, :], w1[:, e:e + 4, :]).then_inc(weights_in, 16)
                sp.dma_start(w2_sb[:, e:e + 4, :, :], w2[:, e:e + 4, :, :]).then_inc(weights_in, 16)

            def steps(i, ffn):
                sp.wait_ge(xn_ready, i + 1)
                sp.dma_start(x_next[:, :], x_rows(x, (i + 1) % NCHUNK)).then_inc(x_next_in, 16)
                if ffn:
                    sp.wait_ge(out_ready, i)
                    sp.dma_start(x_rows(out, i - 1), out_sb[:, :]).then_inc(out_free, 16)
                sp.wait_ge(x1_ready, i + 1)
                sp.dma_start(x_res[:, :], x_rows(x, (i + 1) % NCHUNK)).then_inc(x_res_in, 16)

            steps(0, False)
            with sp.Fori(1, NCHUNK) as i:
                steps(i, True)
            sp.wait_ge(out_ready, NCHUNK)
            sp.dma_start(x_rows(out, NCHUNK - 1), out_sb[:, :]).then_inc(out_free, 16)
            sp.wait_ge(x_next_in, 16 * (NCHUNK + 1))
            sp.wait_ge(x_res_in, 16 * (NCHUNK + 1))
            sp.wait_ge(out_free, 16 * (NCHUNK + 1))

        @block.tensor
        def _(pe):
            mm = nc.tensor.matmul

            def transpose_next(i):
                pe.wait_ge(xn_ready, i + 1)
                nc.tensor.transpose(bank_m[:, 0:P], xn[:, :], ident_sb[:, :]).then_inc(xn_t_done, 1)

            def project(i, g, w, to, done):
                for h in range(HG):
                    last = mm(to[:, h * P:(h + 1) * P], head(w, g * HG + h), h_t[:, :], start=True, stop=True)
                last.then_inc(done, 1)

            def projections(i):
                pe.wait_ge(h_t_ready, i + 1)
                for g in range(G):
                    if g:
                        pe.wait_ge(alpha_ready, i * G + g)
                    elif later(i):
                        pe.wait_ge(k_tok_ready, i * G)
                    project(i, g, wg_sb, bank_a, a_done)
                    if g:
                        pe.wait_ge(k_sq_ready, i * G + g)
                    elif later(i):
                        pe.wait_ge(state_ready, i * G)
                    project(i, g, wk_sb, bank_k, k_done)
                    if g:
                        pe.wait_ge(q_sq_ready, i * G + g)
                    elif later(i):
                        pe.wait_ge(o_t_ready, i * G)
                    project(i, g, wq_sb, bank_q, q_done)

            def norms(i, ffn):
                if ffn:
                    pe.wait_ge(h2_t_ready, i)
                for n, (sq, ready) in enumerate(((k_sq, k_sq_ready), (q_sq, q_sq_ready))):
                    pe.wait_ge(ready, (i + 1) * G)
                    for h in range(H):
                        last = mm(bank_m[:, 256 + n * H + h:257 + n * H + h], head(sq, h), ones_col[:, :],
                                  start=True, stop=True)
                last.then_inc(norms_done, 1)

            def level(i, l, g):
                m = LEVELS[l]
                n = (i * NL + l) * G + g
                if l == 0:
                    if later(i):
                        pe.wait_ge(o_ready, i * G)
                    pe.wait_ge(kd_first, i * G + g + 1)
                else:
                    pe.wait_ge(qd_ready, (i * NU + l - 1) * G + g + 1)
                    if l > 1:
                        pe.wait_ge(kd_ready, (i * (NL - 1) + l - 2) * G + g + 1)
                    pe.wait_ge(scores_ready, n - 1)
                for h in range(HG):
                    if l == 0:
                        last = mm(bank_l[g][:, h * P:(h + 1) * P], head(kd, g * HG + h), head(q_raw, g * HG + h),
                                  start=True, stop=True)
                    else:
                        rhs = head(qd, g * HG + h).rearrange("p (n two m) -> p n two m", two=2, m=m)[:, :, 1, :]
                        last = mm(bank_l[g][:, h * P // 2:(h + 1) * P // 2], head(kd, g * HG + h), rhs,
                                  start=True, stop=True)
                last.then_inc(level_done, 1)

            def values(i, g):
                to = (bank_a, bank_k)[g]
                if g == 0:
                    pe.wait_ge(alpha_ready, (i + 1) * G)
                else:
                    pe.wait_ge(k_sq_ready, (i + 1) * G)
                mm(to[:, :], h_t[:, :], wv_sb[:, cols(g)], start=True, stop=True).then_inc(v_done, 1)

            def keys_by_token(i, g):
                pe.wait_ge(kd_ready, (i * (NL - 1) + NL - 2) * G + g + 1)
                if g == 0:
                    pe.wait_ge(v_ready, (i + 1) * G)
                else:
                    pe.wait_ge(k_tok_ready, i * G + 1)
                for h in range(HG):
                    last = nc.tensor.transpose(bank_a[:, h * P:(h + 1) * P], head(kd, g * HG + h), ident_sb[:, :])
                last.then_inc(k_tok_done, 1)

            def outputs(i, g):
                pe.wait_ge(qd_ready, (i * NU + NU - 1) * G + g + 1)
                pe.wait_ge(scores_ready, (i + 1) * NL * G - G + g + 1)
                if later(i):
                    pe.wait_ge(state_ready, i * G)
                base = (i % B) * (H * P)
                for h in range(g * HG, (g + 1) * HG):
                    at = (h - g * HG) * P
                    mm(bank_l[g][:, at:at + P], head(qd, h), state[:, bass.ds(base + h * P, P)],
                       start=True, stop=False)
                    last = mm(bank_l[g][:, at:at + P], head(scores, h), head(v_sb, h), start=False, stop=True)
                last.then_inc(o_done, 1)

            def updates(i, g):
                pe.wait_ge(k_tok_ready, i * G + g + 1)
                if g:
                    pe.wait_ge(state_ready, i * G + g)
                for h in range(HG):
                    last = mm(bank_k[:, h * P:(h + 1) * P], head(k_tok, g * HG + h), head(v_sb, g * HG + h),
                              start=True, stop=True)
                last.then_inc(update_done, 1)

            def outputs_by_channel(i, g):
                pe.wait_ge(o_ready, i * G + g + 1)
                if g:
                    pe.wait_ge(o_t_ready, i * G + g)
                for h in range(HG):
                    last = nc.tensor.transpose(bank_q[:, h * P:(h + 1) * P], head(o_sb, g * HG + h), ident_sb[:, :])
                last.then_inc(o_t_done, 1)

            def out_projection(i):
                for h in range(H):
                    if h % HG == 0:
                        pe.wait_ge(o_t_ready, i * G + h // HG + 1)
                    last = mm(bank_m[:, 0:D], head(o_t, h), wo_sb[:, h, :], start=(h == 0), stop=(h == H - 1))
                last.then_inc(y_done, 1)

            def ffn_transpose(j):
                pe.wait_ge(xn2_ready, j + 1)
                nc.tensor.transpose(bank_m[:, 0:P], xn2[:, :], ident_sb[:, :]).then_inc(xn2_t_done, 1)

            def ffn_gate(j, j_norms=None):
                pe.wait_ge(h2_t_ready, j + 1)
                if j_norms is not None:
                    pe.wait_ge(sumsq_ready, j_norms + 1)
                mm(bank_m[:, 256:256 + E], h2_t[:, :], gate_w_sb[:, :], start=True, stop=True).then_inc(gate_done, 1)

            def ffn_onehot(j):
                pe.wait_ge(onehot_ready, j + 1)
                nc.tensor.transpose(bank_m[0:E, 0:P], onehot[:, :], ident_sb[:, :]).then_inc(onehot_t_done, 1)

            def ffn_bias(j):
                pe.wait_ge(onehot_t_ready, j + 1)
                mm(bank_m[:, 0:D], onehot_t[:, :], b2_sb[:, :], start=True, stop=True).then_inc(bias_done, 1)

            def ffn_hidden(j, e):
                n = j * E + e
                if e:
                    pe.wait_ge(hid_ready, n)
                for f in range(FC):
                    last = mm(bank_h[:, f * P:(f + 1) * P], w1_sb[:, e, f * P:(f + 1) * P], h2_t[:, :],
                              start=True, stop=True)
                last.then_inc(hid_done, 1)

            def ffn_expert(j, e):
                n = j * E + e
                pe.wait_ge(hid_ready, n + 1)
                if e:
                    pe.wait_ge(acc_ready, j * (E + 1) + e + 1)
                for f in range(FC):
                    last = mm(bank_y[:, 0:D], hid[:, e % 2, f, :], w2_sb[:, e, f, :],
                              start=(f == 0), stop=(f == FC - 1))
                last.then_inc(expert_done, 1)

            def steps(i, ffn):
                projections(i)
                if ffn:
                    ffn_transpose(i - 1)
                norms(i, ffn)
                if ffn:
                    ffn_gate(i - 1, i)
                for l in range(NL):
                    level(i, l, 0)
                    if ffn:
                        if l == 1:
                            ffn_bias(i - 1)
                        ffn_hidden(i - 1, l)
                    level(i, l, 1)
                    if ffn:
                        if l == 0:
                            ffn_onehot(i - 1)
                        else:
                            ffn_expert(i - 1, l - 1)
                    if l == 2:
                        for g in range(G):
                            values(i, g)
                    if l == 4:
                        pe.wait_ge(sumsq_ready, i + 1)
                        if ffn:
                            pe.wait_ge(acc_ready, (i - 1) * (E + 1) + 1)
                        transpose_next(i + 1)
                if ffn:
                    ffn_expert(i - 1, E - 1)
                keys_by_token(i, 0)
                outputs(i, 0)
                keys_by_token(i, 1)
                outputs(i, 1)
                updates(i, 0)
                outputs_by_channel(i, 0)
                updates(i, 1)
                outputs_by_channel(i, 1)
                pe.wait_ge(h_t_ready, i + 2)
                out_projection(i)

            pe.wait_ge(weights_in, 16 * NW)
            pe.wait_ge(setup_dve, 2)
            nc.tensor.transpose(bank_m[:, 0:B], silu_c[:, :], ident_sb[0:B, 0:B]).then_inc(setup_pe, 1)
            pe.wait_ge(setup_dve, 4)
            for n in range(6):
                last = mm(bank_m[:, 64 + n * B:64 + (n + 1) * B], wmod_sb[:, n, :], c_t[:, :], start=True, stop=True)
            last.then_inc(setup_pe, 1)
            for n, part in enumerate((GA, GB)):
                for half in range(2):
                    to = (bank_a, bank_k, bank_q, bank_h)[2 * n + half]
                    for b in range(B // 2):
                        last = mm(to[:, b * D:(b + 1) * D], c_wide[:, half * (B // 2) + b, :], wmod_sb[:, part, :],
                                  start=True, stop=True)
                    last.then_inc(setup_pe, 1)
            pe.wait_ge(setup_dve, 12)
            transpose_next(0)

            steps(0, False)
            with pe.Fori(1, NCHUNK) as i:
                steps(i, True)
            j = NCHUNK - 1
            ffn_transpose(j)
            ffn_gate(j)
            ffn_onehot(j)
            ffn_bias(j)
            for e in range(E):
                ffn_hidden(j, e)
                if e:
                    ffn_expert(j, e - 1)
            ffn_expert(j, E - 1)

        @block.scalar
        def _(act):
            def fn(out_, in_, what, **kw):
                return nc.scalar.activation(out_, in_, what, **kw)

            def attention_in(i):
                for g in range(G):
                    act.wait_ge(a_done, i * G + g + 1)
                    fn(alpha[:, cols(g)], bank_a[:, :], ACT.Sigmoid).then_inc(alpha_ready, 1)
                    act.wait_ge(k_done, i * G + g + 1)
                    fn(kd[:, cols(g)], bank_k[:, :], ACT.Copy).then_inc(kd_first, 1)
                    fn(k_sq[:, cols(g)], bank_k[:, :], ACT.Square).then_inc(k_sq_ready, 1)
                    act.wait_ge(q_done, i * G + g + 1)
                    fn(q_raw[:, cols(g)], bank_q[:, :], ACT.Copy).then_inc(q_raw_ready, 1)
                    fn(q_sq[:, cols(g)], bank_q[:, :], ACT.Square).then_inc(q_sq_ready, 1)

            def values(i, g):
                act.wait_ge(v_done, i * G + g + 1)
                act.wait_ge(rnorm_ready, i + 1)
                src = (bank_a, bank_k)[g]
                for h in range(HG):
                    n = g * HG + h
                    last = fn(head(v_sb, n), src[:, h * P:(h + 1) * P], ACT.Copy, scale=rnorm[:, n:n + 1])
                last.then_inc(v_ready, 1)

            def hidden(j, e):
                act.wait_ge(hid_done, j * E + e + 1)
                for f in range(FC):
                    n = e * FC + f
                    last = fn(hid[:, e % 2, f, :], bank_h[:, f * P:(f + 1) * P], ACT.Relu, bias=b1_sb[:, n:n + 1])
                last.then_inc(hid_ready, 1)

            def steps(i, ffn):
                attention_in(i)
                for l in range(NL):
                    if ffn:
                        hidden(i - 1, l)
                    if l == 2:
                        values(i, 0)
                        values(i, 1)
                for g in range(G):
                    act.wait_ge(k_tok_done, i * G + g + 1)
                    fn(k_tok[:, cols(g)], bank_a[:, :], ACT.Copy).then_inc(k_tok_ready, 1)
                for g in range(G):
                    act.wait_ge(o_t_done, i * G + g + 1)
                    fn(o_t[:, cols(g)], bank_q[:, :], ACT.Copy).then_inc(o_t_ready, 1)

            act.wait_ge(weights_in, 16 * NW)
            fn(silu_c[:, :], c_sb[:, :], ACT.Sigmoid).then_inc(setup_act, 1)
            steps(0, False)
            with act.Fori(1, NCHUNK) as i:
                steps(i, True)
            for e in range(E):
                hidden(NCHUNK - 1, e)

        @block.gpsimd
        def _(pool):
            def rsqrt(out_, in_):
                return nc.gpsimd.tensor_tensor(out_, in_, minus_half[:, 0:in_.shape[1]], ALU.pow)

            def layer_norm_rstd(i, which):
                pool.wait_ge(var_ready, 2 * i + 1 + which)
                rsqrt(rstd[:, which:which + 1], var_eps[:, which:which + 1]).then_inc(rstd_ready, 1)

            def steps(i):
                pool.wait_ge(sumsq_ready, i + 1)
                rsqrt(rnorm[:, :], sumsq[:, :]).then_inc(rnorm_ready, 1)
                for l in range(1, NL):
                    m = LEVELS[l]
                    if l == 1:
                        pool.wait_ge(t_ready, (i + 1))
                    if l == 4:
                        pool.wait_ge(var_ready, 2 * i + 2)
                        rsqrt(rstd[:, 0:1], var_eps[:, 0:1]).then_inc(rstd_ready, 1)
                    for g in range(G):
                        pool.wait_ge(level_done, (i * NL + l) * G + g + 1)
                        left = halves(kd, g, m)[:, :, 0, :]
                        nc.gpsimd.tensor_tensor(left, left, spread(block_products(g, m, 1), m),
                                                ALU.mult).then_inc(kd_ready, 1)
                pool.wait_ge(var_ready, 2 * i + 3)
                rsqrt(rstd[:, 1:2], var_eps[:, 1:2]).then_inc(rstd_ready, 1)

            nc.gpsimd.memset(minus_half[:, :], -0.5).then_inc(setup_pool, 1)
            nc.gpsimd.memset(state[:, :], 0.0).then_inc(setup_pool, 1)
            nc.gpsimd.memset(scores[:, :], 0.0).then_inc(setup_pool, 1)
            pool.wait_ge(setup_pool, 3)
            pool.wait_ge(var_ready, 1)
            rsqrt(rstd[:, 0:1], var_eps[:, 0:1]).then_inc(rstd_ready, 1)
            steps(0)
            with pool.Fori(1, NCHUNK) as i:
                steps(i)

        @block.vector
        def _(dve):
            v = nc.vector
            linked = [0]
            base = [0]

            def link(ins):
                ins.then_inc(dve_step, 1)
                linked[0] += 1
                dve.wait_ge(dve_step, base[0] + linked[0])

            def hold(ins):
                return ins.wait_op(weights_in, 16 * NW, "sem-ge")

            def layer_norm_var(src, which):
                v.bn_stats(stats[:, which, :], src).then_inc(dve_step, 1)
                linked[0] += 1
                dve.wait_ge(dve_step, base[0] + linked[0])
                link(hold(v.bn_aggr(mean_var[:, which, :], stats[:, which, :])))
                v.tensor_scalar(var_eps[:, which:which + 1], mean_var[:, which, 1:2], LN_EPS, None,
                                ALU.add).then_inc(var_ready, 1)

            def layer_norm_scale(to, src, which, ready):
                v.tensor_scalar(to, src, mean_var[:, which, 0:1], rstd[:, which:which + 1],
                                ALU.subtract, ALU.mult).then_inc(ready, 1)

            def modulate(to, i, scale, shift, ready):
                b = i % B
                v.tensor_scalar(to, bank_m[:, 0:P], mod_t[:, scale, bass.ds(b, 1)], mod_t[:, shift, bass.ds(b, 1)],
                                ALU.mult, ALU.add).then_inc(ready, 1)

            def query_update(i, g, l):
                if l == 0:
                    dve.wait_ge(q_raw_ready, i * G + g + 1)
                    v.tensor_tensor(qd[:, cols(g)], q_raw[:, cols(g)], alpha[:, cols(g)],
                                    ALU.mult).then_inc(qd_ready, 1)
                else:
                    m = LEVELS[l]
                    right = halves(qd, g, m)[:, :, 1, :]
                    v.tensor_tensor(right, right, spread(block_products(g, m, 0), m), ALU.mult).then_inc(qd_ready, 1)

            def decay_products(i):
                dve.wait_ge(alpha_ready, (i + 1) * G)
                src, n = alpha[:, :], H * P
                for m in T_AT:
                    n //= 2
                    pair = src.rearrange("p (n two) -> p n two", two=2)
                    dst = t_prod[:, T_AT[m]:T_AT[m] + n]
                    ins = v.tensor_tensor(dst, pair[:, :, 0], pair[:, :, 1], ALU.mult)
                    if m == P:
                        ins.then_inc(t_ready, 1)
                    else:
                        link(ins)
                    src = dst

            def take_scores(i, l, g):
                if l == 0:
                    hold(v.copy_predicated(scores[:, cols(g)], diag_sb[:, :], bank_l[g][:, :])).then_inc(scores_ready, 1)
                else:
                    m = LEVELS[l]
                    by = "p (n m) -> p n m"
                    hold(v.copy_predicated(halves(scores, g, m)[:, :, 1, :],
                                           masks_sb[:, l - 1, :].rearrange(by, m=m),
                                           bank_l[g][:, 0:W // 2].rearrange(by, m=m))).then_inc(scores_ready, 1)

            def choose(j):
                dve.wait_ge(gate_done, j + 1)
                link(v.tensor_tensor(gate_s[:, :], bank_m[:, 256:256 + E], gate_b_sb[:, :], ALU.add))
                link(v.tensor_reduce(gate_max[:, :], gate_s[:, :], AX, ALU.max))
                link(v.scalar_tensor_tensor(gate_rank[:, :], gate_s[:, :], gate_max[:, 0:1], desc_sb[:, :],
                                            ALU.is_equal, ALU.mult))
                link(v.tensor_reduce(gate_first[:, :], gate_rank[:, :], AX, ALU.max))
                ins = v.tensor_scalar(onehot[:, :], gate_rank[:, :], gate_first[:, 0:1], None, ALU.is_equal)
                ins.then_inc(onehot_ready, 1)

            def accumulate(j, e):
                dve.wait_ge(expert_done, j * E + e + 1)
                dve.wait_ge(acc_ready, j * (E + 1) + e + 1)
                v.scalar_tensor_tensor(acc[:, (e + 1) % 2, :], bank_y[:, 0:D], onehot[:, e:e + 1],
                                       acc[:, e % 2, :], ALU.mult, ALU.add).then_inc(acc_ready, 1)

            def finish(j):
                dve.wait_ge(acc_ready, (j + 1) * (E + 1))
                link(v.tensor_tensor(ffn_gated[:, :].unsqueeze(1), acc[:, E % 2, :].unsqueeze(1),
                                     gates[:, 1, bass.ds(j % B, 1), :], ALU.mult))
                dve.wait_ge(out_free, 16 * (j + 1))
                v.tensor_tensor(out_sb[:, :], ffn_gated[:, :], x1[:, :], ALU.add).then_inc(out_ready, 1)

            def ffn_head(j):
                dve.wait_ge(rstd_ready, 2 * j + 3)
                layer_norm_scale(xn2[:, :], x1[:, :], 1, xn2_ready)
                dve.wait_ge(xn2_t_done, j + 1)
                modulate(h2_t[:, :], j, CB, SB, h2_t_ready)

            def ffn_choice_t(j):
                dve.wait_ge(onehot_t_done, j + 1)
                v.tensor_copy(onehot_t[:, :], bank_m[0:E, 0:P]).then_inc(onehot_t_ready, 1)

            def ffn_bias(j):
                dve.wait_ge(bias_done, j + 1)
                v.tensor_copy(acc[:, 0, :], bank_m[:, 0:D]).then_inc(acc_ready, 1)

            def steps(i, ffn):
                if ffn:
                    ffn_head(i - 1)
                for g in range(G):
                    query_update(i, g, 0)
                decay_products(i)
                dve.wait_ge(norms_done, i + 1)
                v.tensor_scalar(sumsq[:, :], bank_m[:, 256:256 + 2 * H], NORM_EPS ** 2, None,
                                ALU.max).then_inc(sumsq_ready, 1)
                if ffn:
                    choose(i - 1)
                for l in range(NL):
                    for g in range(G):
                        dve.wait_ge(level_done, (i * NL + l) * G + g + 1)
                        if l:
                            query_update(i, g, l)
                        take_scores(i, l, g)
                    if ffn:
                        if l == 0:
                            ffn_choice_t(i - 1)
                        if l == 1:
                            ffn_bias(i - 1)
                        if l:
                            accumulate(i - 1, l - 1)
                    if l == 2:
                        dve.wait_ge(x_next_in, 16 * (i + 2))
                        layer_norm_var(x_next[:, :], 0)
                    if l == 3:
                        dve.wait_ge(rstd_ready, 2 * i + 2)
                        layer_norm_scale(xn[:, :], x_next[:, :], 0, xn_ready)
                    if l == 5:
                        dve.wait_ge(xn_t_done, i + 2)
                        modulate(h_t[:, :], i + 1, CA, SA, h_t_ready)
                if ffn:
                    accumulate(i - 1, E - 1)
                    finish(i - 1)
                for g in range(G):
                    dve.wait_ge(o_done, i * G + g + 1)
                    by = "p (h d) -> p h d"
                    rq = rnorm[:, H + g * HG:H + (g + 1) * HG]
                    v.tensor_tensor(o_sb[:, cols(g)].rearrange(by, h=HG), bank_l[g][:, :].rearrange(by, h=HG),
                                    spread(rq, P), ALU.mult).then_inc(o_ready, 1)
                for g in range(G):
                    dve.wait_ge(update_done, i * G + g + 1)
                    for h in range(g * HG, (g + 1) * HG):
                        s = state[:, bass.ds((i % B) * (H * P) + h * P, P)]
                        at = (h - g * HG) * P
                        last = v.scalar_tensor_tensor(s, s, t_prod[:, T_AT[P] + h:T_AT[P] + h + 1],
                                                      bank_k[:, at:at + P], ALU.mult, ALU.add)
                    last.then_inc(state_ready, 1)
                dve.wait_ge(y_done, i + 1)
                link(v.tensor_tensor(y_gated[:, :].unsqueeze(1), bank_m[:, 0:D].unsqueeze(1),
                                     gates[:, 0, bass.ds(i % B, 1), :], ALU.mult))
                dve.wait_ge(x_res_in, 16 * (i + 1))
                v.tensor_tensor(x1[:, :], y_gated[:, :], x_res[:, :], ALU.add).then_inc(x1_ready, 1)
                dve.wait_ge(x1_ready, i + 1)
                layer_norm_var(x1[:, :], 1)

            v.memset(ones_col[:, :], 1.0).then_inc(setup_dve, 1)
            dve.wait_ge(weights_in, 16 * NW)
            dve.wait_ge(setup_act, 1)
            v.tensor_tensor(silu_c[:, :], silu_c[:, :], c_sb[:, :], ALU.mult).then_inc(setup_dve, 1)
            dve.wait_ge(setup_pe, 1)
            v.tensor_copy(c_t[:, :], bank_m[:, 0:B]).then_inc(setup_dve, 1)
            dve.wait_ge(setup_dve, 3)
            v.tensor_copy(c_wide[:, :, :], spread(c_t[:, :], P)).then_inc(setup_dve, 1)
            dve.wait_ge(setup_pe, 2)
            v.tensor_copy(mod_t[:, :, :].rearrange("p a b -> p (a b)"), bank_m[:, 64:64 + 6 * B]).then_inc(setup_dve, 1)
            dve.wait_ge(setup_dve, 5)
            for part in (CA, CB):
                v.tensor_scalar(mod_t[:, part, :], mod_t[:, part, :], 1.0, None, ALU.add).then_inc(setup_dve, 1)
            dve.wait_ge(setup_pe, 6)
            for n in range(2):
                for half in range(2):
                    src = (bank_a, bank_k, bank_q, bank_h)[2 * n + half][:, :].rearrange("p (b d) -> p b d", d=D)
                    at = slice(half * (B // 2), (half + 1) * (B // 2))
                    g = gates[:, n, at, :]
                    link(v.tensor_scalar(gate_sign[:, at, :], src, 0.0, 2.0, ALU.is_ge, ALU.mult))
                    link(v.scalar_tensor_tensor(g, gate_sign[:, at, :], 1.0, src, ALU.subtract, ALU.mult))
                    link(v.tensor_scalar(g, g, GATE_FLOOR, None, ALU.max))
                    v.scalar_tensor_tensor(g, gate_sign[:, at, :], 1.0, g, ALU.subtract, ALU.mult).then_inc(setup_dve, 1)
                if n == 0:
                    dve.wait_ge(setup_dve, 9)
            dve.wait_ge(x_next_in, 16)
            layer_norm_var(x_next[:, :], 0)
            dve.wait_ge(rstd_ready, 1)
            dve.wait_ge(setup_dve, 11)
            v.memset(gate_first[:, :], 0.0).then_inc(setup_dve, 1)
            v.memset(out_sb[:, :], 0.0).then_inc(out_free, 16)
            layer_norm_scale(xn[:, :], x_next[:, :], 0, xn_ready)
            dve.wait_ge(xn_t_done, 1)
            modulate(h_t[:, :], 0, CA, SA, h_t_ready)
            dve.wait_ge(setup_pool, 3)

            steps(0, False)
            before = base[0] + linked[0]
            per_turn = 2 * 2 + 4 + (len(T_AT) - 1) + 1 + 1
            with dve.Fori(1, NCHUNK) as i:
                base[0] = i * per_turn + (before - per_turn)
                linked[0] = 0
                steps(i, True)
                assert linked[0] == per_turn
            base[0] = before + (NCHUNK - 1) * per_turn
            linked[0] = 0
            j = NCHUNK - 1
            ffn_head(j)
            choose(j)
            ffn_choice_t(j)
            ffn_bias(j)
            for e in range(E):
                accumulate(j, e)
            finish(j)


def kernel(**inputs):
    import numpy as np
    import concourse.bacc as bacc
    from concourse.bass_utils import run_bass_kernel_spmd

    a = {k: np.asarray(v) for k, v in inputs.items()}
    s = np.arange(P)[:, None]
    masks = []
    for m in LEVELS[1:]:
        t = np.array([t for t in range(P) if (t // m) % 2])[None, :]
        masks.append(np.tile((s // (2 * m) == t // (2 * m)) & ((s // m) % 2 == 0), (1, HG)))
    arrays = {
        "x": a["L0_attn_x"],
        "wq": a["L0_attn_Wq"], "wk": a["L0_attn_Wk"], "wv": a["L0_attn_Wv"], "wg": a["L0_attn_Wg"],
        "wo": a["L0_attn_Wo"].reshape(H, P, D).transpose(1, 0, 2),
        "gate_w": a["L0_ffn_Wg"],
        "gate_b": np.broadcast_to(a["L0_ffn_bg"], (P, E)),
        "w1": a["L0_ffn_W1"].transpose(1, 0, 2),
        "b1": a["L0_ffn_b1"].reshape(E * FC, P).transpose(1, 0),
        "w2": a["L0_ffn_W2"].reshape(E, FC, P, D).transpose(2, 0, 1, 3),
        "b2": a["L0_ffn_b2"],
        "c": a["L0_c"], "wmod": a["L0_wmod"],
        "ident": np.eye(P, dtype=np.float32),
        "level_masks": np.concatenate(masks, axis=1).astype(np.int32),
        "diag_mask": np.tile(np.eye(P, dtype=np.int32), (1, HG)),
        "descending": np.broadcast_to(np.arange(E, 0, -1, dtype=np.float32), (P, E)),
    }
    nc = bacc.Bacc("TRN2", target_bir_lowering=False, num_devices=1)
    arrays = {k: np.ascontiguousarray(v) for k, v in arrays.items()}
    args = [nc.dram_tensor(k, v.shape, mybir.dt.from_np(v.dtype), kind="ExternalInput").ap()
            for k, v in arrays.items()]
    out = nc.dram_tensor("out", (B, T, D), F32, kind="ExternalOutput").ap()
    adaln_gla_moe(nc, *args, out)
    r = run_bass_kernel_spmd(nc, [arrays], core_ids=[0])
    return r.results[0]["out"]
```

```python
from contextlib import ExitStack

import concourse.bass as bass
from concourse import mybir

F32 = mybir.dt.float32
I32 = mybir.dt.int32
ALU = mybir.AluOpType
ACT = mybir.ActivationFunctionType
AX = mybir.AxisListType.X

P = 128
B, T, D = 8, 1024, 128
H = 8
E, F = 8, 512
FC = F // P
NCHUNK = B * T // P
STEPS = [1, 2, 4, 8, 16, 32, 64]
NS = len(STEPS)
NEAR = 5
Q = 32
G = 2
HG = H // G
W = HG * P
LN_EPS = 1e-5
NORM_EPS = 1e-12
GATE_FLOOR = 0.25
SA, CA, GA, SB, CB, GB = range(6)
T_AT = {}
for _m in (2, 4, 8, 16, 32, 64, 128):
    T_AT[_m] = sum(H * P // n for n in T_AT)
T_LEN = sum(H * P // n for n in T_AT)

ORDER = [
    ("first", 0), ("hidden", 0), ("first", 1), ("keys_tok", 0), ("choice",), ("first", 2), ("hidden", 1),
    ("first", 3), ("keys_tok", 1), ("bias",),
    ("level", 1, 0), ("outputs", 0), ("level", 1, 1), ("expert", 0), ("hidden", 2),
    ("level", 2, 0), ("outputs", 1), ("level", 2, 1), ("updates", 0), ("expert", 1),
    ("level", 3, 0), ("updates", 1), ("hidden", 3), ("level", 3, 1), ("a", 0), ("expert", 2),
    ("residual",),
    ("level", 4, 0), ("k", 0), ("hidden", 4), ("level", 4, 1), ("q", 0), ("expert", 3),
    ("level", 5, 0), ("a", 1), ("hidden", 5), ("level", 5, 1), ("k", 1), ("expert", 4), ("norm2",),
    ("level", 6, 0), ("q", 1), ("hidden", 6), ("level", 6, 1), ("expert", 5), ("norms", 0), ("hidden", 7),
    ("values", 0), ("norms", 1), ("expert", 6), ("channels2",), ("values", 1), ("channels",), ("expert", 7),
    ("gate",),
]
OWN, TAIL, NEXT, EXPERTS = "own", "tail", "next", "experts"
PART = {"first": OWN, "level": OWN, "keys_tok": TAIL, "outputs": TAIL, "updates": TAIL, "channels2": TAIL,
        "residual": TAIL, "norm2": TAIL,
        "gate": TAIL, "a": NEXT, "k": NEXT, "q": NEXT, "values": NEXT, "norms": NEXT, "channels": NEXT,
        "choice": EXPERTS, "bias": EXPERTS, "hidden": EXPERTS, "expert": EXPERTS}
ALL = (OWN, TAIL, NEXT, EXPERTS)
CHAINED = {OWN: 0, TAIL: 7, NEXT: 12, EXPERTS: 1}
PROLOGUE = [(-1, (NEXT,)), (0, (OWN, NEXT)), (1, (OWN, TAIL, NEXT))]
EPILOGUE = [(NCHUNK, (TAIL, EXPERTS)), (NCHUNK + 1, (EXPERTS,))]


def adaln_gla_moe(nc, x, wq, wk, wv, wg, wo, gate_w, gate_b, w1, b1, w2, b2, c, wmod,
                  ident, fold, level_masks, diag_mask, descending, out):
    with ExitStack() as ctx:
        def sb(name, shape, dt=F32):
            return ctx.enter_context(nc.sbuf_tensor(name, shape, dt))

        def bank(name):
            return ctx.enter_context(nc.psum_tensor(name, [P, 512], F32))

        def sem(name):
            return ctx.enter_context(nc.semaphore(name))

        wq_sb, wk_sb, wvo_sb, wg_sb = (sb(f"w{n}_sb", [P, H * P]) for n in ("q", "k", "vo", "g"))
        w1_sb = sb("w1_sb", [P, E, F])
        w2_sb = sb("w2_sb", [P, E, FC, D])
        b1_sb = sb("b1_sb", [P, E * FC])
        b2_sb = sb("b2_sb", [E, D])
        gate_w_sb = sb("gate_w_sb", [P, E])
        gate_b_sb = sb("gate_b_sb", [P, E])
        ident_sb = sb("ident_sb", [P, P])
        masks_sb = sb("masks_sb", [P, NEAR, W // 2], I32)
        fold_sb = sb("fold_sb", [P, Q])
        diag_sb = sb("diag_sb", [P, 2 * P], I32)
        desc_sb = sb("desc_sb", [P, E])
        minus_half = sb("minus_half", [P, H])
        c_sb = sb("c_sb", [B, P])
        silu_c = sb("silu_c", [B, P])
        c_t = sb("c_t", [P, B])
        c_wide = sb("c_wide", [P, B, P])
        wmod_sb = sb("wmod_sb", [P, 6, D])
        mod_t = sb("mod_t", [P, 6, B])
        gates = sb("gates", [P, 2, B, D])
        state = sb("state", [P, B * H * P])
        def twice(name, shape):
            return [sb(f"{name}{n}", shape) for n in range(2)]

        alphas, qds, kds, scoress, vs = (twice(n, [P, H * P]) for n in ("alpha", "qd", "kd", "scores", "v"))
        t_prods = twice("t_prod", [P, T_LEN])
        x1s = twice("x1_", [P, D])
        h2_ts = twice("h2_t", [P, P])
        rq_norms = twice("rq_norm", [P, H])
        rk_norm = sb("rk_norm", [P, H])
        x_next = sb("x_next", [P, D])
        x_res = sb("x_res", [P, D])
        stats = sb("stats", [P, 2, 6])
        mean_var = sb("mean_var", [P, 2, 2])
        var_eps = sb("var_eps", [P, 2])
        rstd = sb("rstd", [P, 2])
        xn = sb("xn", [P, D])
        xn2 = sb("xn2", [P, D])
        h_t = sb("h_t", [P, P])
        q_first = sb("q_first", [P, H, P + P // 2])
        q_sq = sb("q_sq", [P, H * P])
        k_sq = sb("k_sq", [P, H * P])
        k_tok = sb("k_tok", [P, H * P])
        o_sb = sb("o_sb", [P, H * P])
        o_pairs = sb("o_pairs", [P, 6 * D])
        y_sb = sb("y_sb", [P, D])
        sq_t = sb("sq_t", [P, W])
        sq_sums = sb("sq_sums", [P, 2, H * P // Q])
        sumsq = sb("sumsq", [P, 2 * H])
        y_gated = sb("y_gated", [P, D])
        gate_s = sb("gate_s", [P, E])
        gate_max = sb("gate_max", [P, 1])
        gate_rank = sb("gate_rank", [P, E])
        gate_first = sb("gate_first", [P, 1])
        onehot = sb("onehot", [P, E])
        onehot_t = sb("onehot_t", [E, P])
        hid = sb("hid", [P, 2, FC, P])
        acc = sb("acc", [P, 2, D])
        ffn_gated = sb("ffn_gated", [P, D])
        out_sb = sb("out_sb", [P, D])

        bank_a = bank("bank_a")
        bank_k = bank("bank_k")
        bank_q = bank("bank_q")
        bank_l = [bank("bank_l0"), bank("bank_l1")]
        bank_m = bank("bank_m")
        bank_h = bank("bank_h")
        bank_y = bank("bank_y")

        weights_in = sem("weights_in")
        x_next_in = sem("x_next_in")
        x_res_in = sem("x_res_in")
        out_free = sem("out_free")
        setup_dve = sem("setup_dve")
        setup_pe = sem("setup_pe")
        setup_act = sem("setup_act")
        setup_pool = sem("setup_pool")
        a_done, k_done, q_done, v_done = (sem(f"{n}_done") for n in "akqv")
        norms_done = sem("norms_done")
        level_done = sem("level_done")
        wv_t_done = sem("wv_t_done")
        k_tok_done = sem("k_tok_done")
        o_done = sem("o_done")
        update_done = sem("update_done")
        xn_t_done = sem("xn_t_done")
        xn2_t_done = sem("xn2_t_done")
        gate_done = sem("gate_done")
        onehot_t_done = sem("onehot_t_done")
        bias_done = sem("bias_done")
        hid_done = sem("hid_done")
        expert_done = sem("expert_done")
        alpha_ready = sem("alpha_ready")
        kd_first = sem("kd_first")
        k_sq_ready = sem("k_sq_ready")
        q_raw_ready = sem("q_raw_ready")
        q_sq_ready = sem("q_sq_ready")
        v_ready = sem("v_ready")
        k_tok_ready = sem("k_tok_ready")
        far_ready = sem("far_ready")
        sq_sums_ready = sem("sq_sums_ready")
        y_ready = sem("y_ready")
        pool_step = sem("pool_step")
        hid_ready = sem("hid_ready")
        q_first_ready = sem("q_first_ready")
        qd_ready = sem("qd_ready")
        kd_ready = sem("kd_ready")
        t_ready = sem("t_ready")
        scores_ready = sem("scores_ready")
        sumsq_ready = sem("sumsq_ready")
        rnorm_ready = sem("rnorm_ready")
        var_ready, var2_ready = sem("var_ready"), sem("var2_ready")
        rstd_ready, rstd2_ready = sem("rstd_ready"), sem("rstd2_ready")
        xn_ready = sem("xn_ready")
        xn2_ready = sem("xn2_ready")
        h_t_ready = sem("h_t_ready")
        h2_t_ready = sem("h2_t_ready")
        onehot_ready = sem("onehot_ready")
        onehot_t_ready = sem("onehot_t_ready")
        acc_ready = sem("acc_ready")
        o_ready = sem("o_ready")
        state_ready = sem("state_ready")
        x1_ready = sem("x1_ready")
        out_ready = sem("out_ready")
        dve_step = sem("dve_step")

        LEVELS_DONE = 2 * G + (NS - 1) * G
        NEAR_READS = (4 + NEAR - 1) * G
        NW = 20

        def x_rows(tensor, i):
            return tensor[bass.ds(i % B, 1), bass.ds((i // B) * P, P), :].rearrange("a t d -> (a t) d")

        def cols(g):
            return slice(g * W, (g + 1) * W)

        def head(buf, h):
            return buf[:, h * P:(h + 1) * P]

        def q_first_signal(i, l, g):
            return i * (2 * G) + 2 * g + l + 1

        def q_signal(i, l, g):
            return (i * (NS - 1) + l - 2) * G + g + 1

        def k_signal(i, l, g):
            return (i * NS + l - 1) * G + g + 1

        def pair_done(i, pair):
            return i * LEVELS_DONE + pair + 1

        def step_done(i, l, g):
            return i * LEVELS_DONE + 2 * G + (l - 1) * G + g + 1

        def near_read(i, l, g):
            at = 2 * (G + g + 1) if l == 0 else 4 * G + (l - 1) * G + g + 1
            return i * NEAR_READS + at

        def far_read(i, l, g):
            return (i * (NS - NEAR) + l - NEAR) * G + g + 1

        def halves(buf, g, m):
            return buf[:, cols(g)].rearrange("p (n two m) -> p n two m", two=2, m=m)

        def block_products(par, g, m, side):
            n = W // m
            buf = alphas[par][:, cols(g)] if m == 1 else t_prods[par][:, T_AT[m] + g * n:T_AT[m] + (g + 1) * n]
            return buf.rearrange("p (n two) -> p n two", two=2)[:, :, side]

        def slots(engine, slot):
            for i, parts in PROLOGUE:
                slot(i, i % 2, parts)
            with engine.Fori(1, NCHUNK // 2) as n:
                for par in range(2):
                    slot(n * 2 + par, par, ALL)
            for i, parts in EPILOGUE:
                slot(i, i % 2, parts)

        def spread(ap, m):
            return ap.unsqueeze(2).broadcast_to((P, ap.shape[1], m))

        block = ctx.enter_context(nc.Block())

        @block.sync
        def _(sp):
            loads = [(c_sb[:, :], c), (wmod_sb[:, :, :].rearrange("p a b -> p (a b)"), wmod),
                     (ident_sb[:, :], ident), (wg_sb[:, :], wg), (wk_sb[:, :], wk), (wq_sb[:, :], wq),
                     (vs[0][:, :], wv), (k_tok[:, :], wo), (fold_sb[:, :], fold), (masks_sb[:, :, :].rearrange("p a b -> p (a b)"), level_masks),
                     (diag_sb[:, :], diag_mask), (gate_w_sb[:, :], gate_w),
                     (gate_b_sb[:, :], gate_b), (desc_sb[:, :], descending), (b1_sb[:, :], b1),
                     (b2_sb[:, :], b2)]
            sp.dma_start(x_next[:, :], x_rows(x, 0)).then_inc(x_next_in, 16)
            sp.dma_start(x_res[:, :], x_rows(x, 0)).then_inc(x_res_in, 16)
            for to, of in loads:
                sp.dma_start(to, of).then_inc(weights_in, 16)
            for e in range(0, E, 4):
                sp.dma_start(w1_sb[:, e:e + 4, :], w1[:, e:e + 4, :]).then_inc(weights_in, 16)
                sp.dma_start(w2_sb[:, e:e + 4, :, :], w2[:, e:e + 4, :, :]).then_inc(weights_in, 16)

            def slot(i, par, parts):
                if NEXT in parts:
                    sp.wait_ge(xn_ready, i + 3)
                    sp.dma_start(x_next[:, :], x_rows(x, (i + 3) % NCHUNK)).then_inc(x_next_in, 16)
                if TAIL in parts:
                    sp.wait_ge(x1_ready, i)
                    sp.dma_start(x_res[:, :], x_rows(x, i % NCHUNK)).then_inc(x_res_in, 16)
                if EXPERTS in parts:
                    sp.wait_ge(out_ready, i - 1)
                    sp.dma_start(x_rows(out, i - 2), out_sb[:, :]).then_inc(out_free, 16)

            sp.wait_ge(xn_ready, 1)
            sp.dma_start(x_next[:, :], x_rows(x, 1)).then_inc(x_next_in, 16)
            slots(sp, slot)
            sp.wait_ge(x_next_in, 16 * (NCHUNK + 3))
            sp.wait_ge(x_res_in, 16 * (NCHUNK + 1))
            sp.wait_ge(out_free, 16 * (NCHUNK + 1))

        @block.tensor
        def _(pe):
            mm = nc.tensor.matmul

            def transpose_input(c):
                pe.wait_ge(xn_ready, c + 1)
                nc.tensor.transpose(bank_m[:, 0:P], xn[:, :], ident_sb[:, :]).then_inc(xn_t_done, 1)

            def project(g, w, to, done):
                for h in range(HG):
                    last = mm(to[:, h * P:(h + 1) * P], head(w, g * HG + h), h_t[:, :], start=True, stop=True)
                last.then_inc(done, 1)

            def projection(c, which, g, tail):
                if which == "a":
                    if g:
                        pe.wait_ge(alpha_ready, c * G + 1)
                    else:
                        pe.wait_ge(h_t_ready, c + 1)
                        if tail:
                            pe.wait_ge(o_ready, (c - 1) * G)
                        elif c:
                            pe.wait_ge(v_ready, c * G)
                    project(g, wg_sb, bank_a, a_done)
                elif which == "k":
                    if g:
                        pe.wait_ge(k_sq_ready, c * G + 1)
                    elif tail:
                        pe.wait_ge(state_ready, (c - 2) * G + 1)
                    elif c:
                        pe.wait_ge(v_ready, c * G)
                    project(g, wk_sb, bank_k, k_done)
                else:
                    if g:
                        pe.wait_ge(q_sq_ready, c * G + 1)
                    elif tail:
                        pe.wait_ge(state_ready, (c - 1) * G)
                    elif c:
                        pe.wait_ge(q_sq_ready, c * G)
                    project(g, wq_sb, bank_q, q_done)

            def fold_norms(c, which, experts):
                if which:
                    pe.wait_ge(sumsq_ready, 2 * c + 1)
                elif experts:
                    pe.wait_ge(acc_ready, (c - 3) * (E + 1) + 1)
                pe.wait_ge(sq_sums_ready, c * 2 * G + 2 * G - 1 + which)
                for n in range(P // Q):
                    last = mm(bank_m[n * Q:(n + 1) * Q, 256:256 + H], fold_sb[:, :],
                              sq_sums[:, which, :].rearrange("p (h n) -> p n h", n=P // Q)[:, n, :],
                              start=True, stop=True)
                last.then_inc(norms_done, 1)

            def first(i, par, pair):
                g = pair // 2
                to = bank_l[pair % 2]
                if pair >= 2:
                    pe.wait_ge(scores_ready, i * NEAR_READS + 2 * (pair - 1))
                elif not isinstance(i, int) or i:
                    pe.wait_ge(far_ready, far_read(i - 1, NS - 1, pair))
                pe.wait_ge(k_sq_ready, i * G + g + 1)
                pe.wait_ge(q_first_ready, q_first_signal(i, 0, g))
                for n in range(2):
                    h = pair * 2 + n
                    at = n * (P + P // 2)
                    last = mm(to[:, at:at + P + P // 2], head(kds[par], h), q_first[:, h, :], start=True, stop=True)
                last.then_inc(level_done, 1)

            def level(i, par, l, g):
                m = STEPS[l]
                if l == 1:
                    pe.wait_ge(q_first_ready, q_first_signal(i, l, g))
                else:
                    pe.wait_ge(qd_ready, q_signal(i, l, g))
                pe.wait_ge(kd_ready, k_signal(i, l, g))
                if l <= NEAR:
                    pe.wait_ge(scores_ready, near_read(i, l - 1, g))
                else:
                    pe.wait_ge(far_ready, far_read(i, l - 1, g))
                for h in range(g * HG, (g + 1) * HG):
                    k, q, n = head(kds[par], h), head(qds[par], h), h - g * HG
                    if l < NEAR:
                        rhs = q.rearrange("p (n two m) -> p n two m", two=2, m=m)[:, :, 1, :]
                        last = mm(bank_l[g][:, n * P // 2:(n + 1) * P // 2], k, rhs, start=True, stop=True)
                    else:
                        for at in range(0, P, 2 * m):
                            last = mm(bank_l[g][at:at + m, n * m:(n + 1) * m], k[:, at:at + m],
                                      q[:, at + m:at + 2 * m], start=True, stop=True)
                last.then_inc(level_done, 1)

            def values(c, g):
                if g == 0:
                    pe.wait_ge(alpha_ready, (c + 1) * G)
                else:
                    pe.wait_ge(k_sq_ready, (c + 1) * G)
                mm((bank_a, bank_k)[g][:, :], h_t[:, :], wvo_sb[:, cols(g)], start=True, stop=True).then_inc(v_done, 1)

            def keys_tok(c, par, g):
                pe.wait_ge(kd_ready, k_signal(c, NS, g))
                pe.wait_ge(v_ready, (c + 2) * G)
                for h in range(HG):
                    last = nc.tensor.transpose((bank_a, bank_k)[g][:, h * P:(h + 1) * P], head(kds[par], g * HG + h),
                                               ident_sb[:, :])
                last.then_inc(k_tok_done, 1)

            def outputs(c, par, g):
                pe.wait_ge(qd_ready, q_signal(c, NS, g))
                pe.wait_ge(scores_ready, near_read(c, NEAR - 1, g))
                pe.wait_ge(far_ready, far_read(c, NS - 1, g))
                if not isinstance(c, int) or c:
                    pe.wait_ge(state_ready, c * G)
                if g:
                    pe.wait_ge(k_tok_ready, c * G + 1)
                else:
                    pe.wait_ge(q_sq_ready, (c + 2) * G)
                to = (bank_q, bank_a)[g]
                base = (c % B) * (H * P)
                for h in range(g * HG, (g + 1) * HG):
                    at = (h - g * HG) * P
                    mm(to[:, at:at + P], head(qds[par], h), state[:, bass.ds(base + h * P, P)],
                       start=True, stop=False)
                    last = mm(to[:, at:at + P], head(scoress[par], h), head(vs[par], h), start=False, stop=True)
                last.then_inc(o_done, 1)

            def updates(c, par, g):
                pe.wait_ge(k_tok_ready, (c + 1) * G)
                if g:
                    pe.wait_ge(o_ready, c * G + 1)
                for h in range(HG):
                    last = mm((bank_k, bank_q)[g][:, h * P:(h + 1) * P], head(k_tok, g * HG + h),
                              head(vs[par], g * HG + h), start=True, stop=True)
                last.then_inc(update_done, 1)

            def channels2(c, nxt):
                if nxt:
                    pe.wait_ge(sumsq_ready, 2 * (c + 2) + 2)
                else:
                    pe.wait_ge(acc_ready, (c - 1) * (E + 1) + 1)
                pe.wait_ge(xn2_ready, c + 1)
                nc.tensor.transpose(bank_m[:, 0:P], xn2[:, :], ident_sb[:, :]).then_inc(xn2_t_done, 1)

            def channels(c, tail):
                if tail:
                    pe.wait_ge(h2_t_ready, c - 2)
                else:
                    pe.wait_ge(sumsq_ready, 2 * (c - 1) + 2)
                transpose_input(c)

            def gate(c, par, nxt):
                pe.wait_ge(h2_t_ready, c + 1)
                if nxt:
                    pe.wait_ge(h_t_ready, c + 4)
                mm(bank_m[:, 256:256 + E], h2_ts[par][:, :], gate_w_sb[:, :], start=True, stop=True).then_inc(gate_done, 1)

            def choice(j):
                pe.wait_ge(onehot_ready, j + 1)
                nc.tensor.transpose(bank_m[0:E, 0:P], onehot[:, :], ident_sb[:, :]).then_inc(onehot_t_done, 1)

            def bias(j):
                pe.wait_ge(onehot_t_ready, j + 1)
                mm(bank_m[:, 0:D], onehot_t[:, :], b2_sb[:, :], start=True, stop=True).then_inc(bias_done, 1)

            def hidden(j, par, e):
                n = j * E + e
                if e:
                    pe.wait_ge(hid_ready, n)
                for f in range(FC):
                    last = mm(bank_h[:, f * P:(f + 1) * P], w1_sb[:, e, f * P:(f + 1) * P], h2_ts[par][:, :],
                              start=True, stop=True)
                last.then_inc(hid_done, 1)

            def expert(j, e):
                pe.wait_ge(hid_ready, j * E + e + 1)
                pe.wait_ge(acc_ready, j * (E + 1) + e + 1)
                for f in range(FC):
                    last = mm(bank_y[:, 0:D], hid[:, e % 2, f, :], w2_sb[:, e, f, :],
                              start=(f == 0), stop=(f == FC - 1))
                last.then_inc(expert_done, 1)

            def slot(i, par, parts):
                tail, nxt = TAIL in parts, NEXT in parts
                for what, *n in ORDER:
                    if PART[what] not in parts:
                        continue
                    if what == "first":
                        first(i, par, *n)
                    elif what == "level":
                        level(i, par, *n)
                    elif what in ("a", "k", "q"):
                        projection(i + 1, what, n[0], tail)
                    elif what == "norms":
                        fold_norms(i + 1, n[0], EXPERTS in parts)
                    elif what == "values":
                        values(i + 1, *n)
                    elif what == "channels":
                        channels(i + 2, tail)
                    elif what == "keys_tok":
                        keys_tok(i - 1, 1 - par, *n)
                    elif what == "outputs":
                        outputs(i - 1, 1 - par, *n)
                    elif what == "updates":
                        updates(i - 1, 1 - par, *n)
                    elif what == "channels2":
                        channels2(i - 1, nxt)
                    elif what == "gate":
                        gate(i - 1, 1 - par, nxt)
                    elif what == "choice":
                        choice(i - 2)
                    elif what == "bias":
                        bias(i - 2)
                    elif what == "hidden":
                        hidden(i - 2, par, *n)
                    elif what == "expert":
                        expert(i - 2, *n)

            pe.wait_ge(weights_in, 16 * NW)
            pe.wait_ge(setup_dve, 1)
            nc.tensor.transpose(bank_m[:, 0:B], silu_c[:, :], ident_sb[0:B, 0:B]).then_inc(setup_pe, 1)
            pe.wait_ge(setup_dve, 3)
            for n in range(6):
                last = mm(bank_m[:, 64 + n * B:64 + (n + 1) * B], wmod_sb[:, n, :], c_t[:, :], start=True, stop=True)
            last.then_inc(setup_pe, 1)
            for n, part in enumerate((GA, GB)):
                for half in range(2):
                    to = (bank_a, bank_k, bank_q, bank_h)[2 * n + half]
                    for b in range(B // 2):
                        last = mm(to[:, b * D:(b + 1) * D], c_wide[:, half * (B // 2) + b, :], wmod_sb[:, part, :],
                                  start=True, stop=True)
                    last.then_inc(setup_pe, 1)
            pe.wait_ge(setup_dve, 10)
            for h in range(H):
                to = (bank_a, bank_k)[h // HG]
                at = h % HG * P
                last = nc.tensor.transpose(to[:, at:at + P], head(vs[0], h), ident_sb[:, :])
            last.then_inc(wv_t_done, 1)
            pe.wait_ge(setup_dve, 12)
            for h in range(H):
                to = (bank_q, bank_h)[h // HG]
                at = h % HG * P
                last = mm(to[:, at:at + P], head(o_sb, h), head(k_tok, h), start=True, stop=True)
            last.then_inc(setup_pe, 1)
            transpose_input(0)
            pe.wait_ge(setup_dve, 13)
            pe.wait_ge(setup_pool, 4)
            slots(pe, slot)

        @block.scalar
        def _(act):
            def fn(out_, in_, what, **kw):
                return nc.scalar.activation(out_, in_, what, **kw)

            def projection(c, par, which, g):
                hs = slice(g * HG, (g + 1) * HG)
                if which == "a":
                    act.wait_ge(a_done, c * G + g + 1)
                    fn(alphas[par][:, cols(g)], bank_a[:, :], ACT.Sigmoid).then_inc(alpha_ready, 1)
                elif which == "k":
                    act.wait_ge(k_done, c * G + g + 1)
                    fn(kds[par][:, cols(g)], bank_k[:, :], ACT.Copy)
                    fn(k_sq[:, cols(g)], bank_k[:, :], ACT.Square).then_inc(k_sq_ready, 1)
                else:
                    act.wait_ge(q_done, c * G + g + 1)
                    fn(q_first[:, hs, 0:P], bank_q[:, :].rearrange("p (h t) -> p h t", h=HG),
                       ACT.Copy).then_inc(q_raw_ready, 1)
                    fn(q_sq[:, cols(g)], bank_q[:, :], ACT.Square).then_inc(q_sq_ready, 1)

            def values(c, par, g):
                act.wait_ge(v_done, c * G + g + 1)
                act.wait_ge(rnorm_ready, 2 * c + 1)
                src = (bank_a, bank_k)[g]
                for h in range(HG):
                    n = g * HG + h
                    last = fn(head(vs[par], n), src[:, h * P:(h + 1) * P], ACT.Copy, scale=rk_norm[:, n:n + 1])
                last.then_inc(v_ready, 1)

            def hidden(j, e):
                act.wait_ge(hid_done, j * E + e + 1)
                for f in range(FC):
                    n = e * FC + f
                    last = fn(hid[:, e % 2, f, :], bank_h[:, f * P:(f + 1) * P], ACT.Relu, bias=b1_sb[:, n:n + 1])
                last.then_inc(hid_ready, 1)

            def far_scores(i, par, l, g):
                m = STEPS[l]
                act.wait_ge(level_done, step_done(i, l, g))
                to = scoress[par][:, cols(g)].rearrange("p (h t) -> p h t", h=HG)
                for at in range(0, P, 2 * m):
                    last = fn(to[at:at + m, :, at + m:at + 2 * m],
                              bank_l[g][at:at + m, 0:HG * m].rearrange("p (h t) -> p h t", h=HG), ACT.Copy)
                last.then_inc(far_ready, 1)

            def keys_tok(c, g):
                act.wait_ge(k_tok_done, c * G + g + 1)
                fn(k_tok[:, cols(g)], (bank_a, bank_k)[g][:, :], ACT.Copy).then_inc(k_tok_ready, 1)

            def slot(i, par, parts):
                for what, *n in ORDER:
                    if PART[what] not in parts:
                        continue
                    if what == "level" and n[0] >= NEAR:
                        far_scores(i, par, *n)
                    elif what in ("a", "k", "q"):
                        projection(i + 1, 1 - par, what, *n)
                    elif what == "values":
                        values(i + 1, 1 - par, *n)
                    elif what == "keys_tok":
                        keys_tok(i - 1, *n)
                    elif what == "hidden":
                        hidden(i - 2, *n)

            act.wait_ge(weights_in, 16 * NW)
            fn(silu_c[:, :], c_sb[:, :], ACT.Sigmoid).then_inc(setup_act, 1)
            slots(act, slot)

        @block.gpsimd
        def _(pool):
            def rsqrt(out_, in_):
                return nc.gpsimd.tensor_tensor(out_, in_, minus_half[:, 0:in_.shape[1]], ALU.pow)

            def norm(c, par, which):
                pool.wait_ge(sumsq_ready, 2 * c + which + 1)
                to = (rk_norm, rq_norms[par])[which]
                rsqrt(to[:, :], sumsq[:, which * H:(which + 1) * H]).then_inc(rnorm_ready, 1)

            def layer_norm(which, n):
                pool.wait_ge((var_ready, var2_ready)[which], n)
                rsqrt(rstd[:, which:which + 1], var_eps[:, which:which + 1]).then_inc((rstd_ready, rstd2_ready)[which], 1)

            def add_heads(c):
                pool.wait_ge(o_ready, (c + 1) * G)
                half, quarter = o_pairs[:, 0:4 * D], o_pairs[:, 4 * D:6 * D]
                nc.gpsimd.tensor_tensor(half, o_sb[:, 0:4 * D], o_sb[:, 4 * D:8 * D], ALU.add).then_inc(pool_step, 1)
                pool.wait_ge(pool_step, 2 * c + 1)
                nc.gpsimd.tensor_tensor(quarter, half[:, 0:2 * D], half[:, 2 * D:4 * D], ALU.add).then_inc(pool_step, 1)
                pool.wait_ge(pool_step, 2 * c + 2)
                nc.gpsimd.tensor_tensor(y_sb[:, :], quarter[:, 0:D], quarter[:, D:2 * D], ALU.add).then_inc(y_ready, 1)

            def key_update(i, par, l, g):
                pool.wait_ge(level_done, step_done(i, l, g) if l else pair_done(i, 2 * g + 1))
                left = halves(kds[par], g, STEPS[l])[:, :, 0, :]
                nc.gpsimd.tensor_tensor(left, left, spread(block_products(par, g, STEPS[l], 1), STEPS[l]),
                                        ALU.mult).then_inc(kd_ready, 1)

            def slot(i, par, parts):
                if OWN in parts:
                    pool.wait_ge(t_ready, i + 1)
                if NEXT in parts:
                    layer_norm(0, i + 3)
                for what, *n in ORDER:
                    if PART[what] not in parts:
                        continue
                    if what == "first" and n[0] % 2:
                        key_update(i, par, 0, n[0] // 2)
                    elif what == "level":
                        key_update(i, par, *n)
                    elif what == "norms":
                        norm(i + 1, 1 - par, *n)
                    elif what == "updates" and n[0]:
                        add_heads(i - 1)
                        layer_norm(1, i)

            nc.gpsimd.memset(minus_half[:, :], -0.5).then_inc(setup_pool, 1)
            nc.gpsimd.memset(state[:, :], 0.0).then_inc(setup_pool, 1)
            for n in range(2):
                nc.gpsimd.memset(scoress[n][:, :], 0.0).then_inc(setup_pool, 1)
            pool.wait_ge(setup_pool, 4)
            layer_norm(0, 1)
            slots(pool, slot)

        @block.vector
        def _(dve):
            v = nc.vector
            linked = [0]
            base = [0]

            def link(ins):
                ins.then_inc(dve_step, 1)
                linked[0] += 1
                dve.wait_ge(dve_step, base[0] + linked[0])

            def chain_start(i):
                outside = [(n, parts) for n, parts in PROLOGUE + EPILOGUE if n < (i if isinstance(i, int) else 2)]
                steps = in_setup + sum(CHAINED[part] for _, parts in outside for part in parts)
                turns = NCHUNK - 2 if isinstance(i, int) and i >= NCHUNK else 0 if isinstance(i, int) else i - 2
                return turns * sum(CHAINED.values()) + steps

            def hold(ins):
                return ins.wait_op(weights_in, 16 * NW, "sem-ge")

            def layer_norm_var(src, which):
                v.bn_stats(stats[:, which, :], src).then_inc(dve_step, 1)
                linked[0] += 1
                dve.wait_ge(dve_step, base[0] + linked[0])
                link(hold(v.bn_aggr(mean_var[:, which, :], stats[:, which, :])))
                v.tensor_scalar(var_eps[:, which:which + 1], mean_var[:, which, 1:2], LN_EPS, None,
                                ALU.add).then_inc((var_ready, var2_ready)[which], 1)

            def layer_norm_scale(to, src, which, ready):
                v.tensor_scalar(to, src, mean_var[:, which, 0:1], rstd[:, which:which + 1],
                                ALU.subtract, ALU.mult).then_inc(ready, 1)

            def modulate(to, i, scale, shift, ready):
                b = i % B
                v.tensor_scalar(to, bank_m[:, 0:P], mod_t[:, scale, bass.ds(b, 1)], mod_t[:, shift, bass.ds(b, 1)],
                                ALU.mult, ALU.add).then_inc(ready, 1)

            def first_queries(c, par, g):
                dve.wait_ge(q_raw_ready, c * G + g + 1)
                dve.wait_ge(alpha_ready, c * G + g + 1)
                hs = slice(g * HG, (g + 1) * HG)
                q = q_first[:, hs, 0:P].rearrange("p h (n two) -> p h n two", two=2)
                a = alphas[par][:, cols(g)].rearrange("p (h n two) -> p h n two", h=HG, two=2)
                to = qds[par][:, cols(g)].rearrange("p (h n two) -> p h n two", h=HG, two=2)
                odd = q_first[:, hs, P:P + P // 2]
                v.tensor_tensor(odd, q[:, :, :, 1], a[:, :, :, 1], ALU.mult).then_inc(q_first_ready, 1)
                v.tensor_tensor(to[:, :, :, 0], q[:, :, :, 0], a[:, :, :, 0], ALU.mult)
                dve.wait_ge(q_first_ready, q_first_signal(c, 0, g))
                v.tensor_tensor(to[:, :, :, 1], odd, a[:, :, :, 0], ALU.mult).then_inc(q_first_ready, 1)

            def query_update(par, g, l):
                m = STEPS[l]
                right = halves(qds[par], g, m)[:, :, 1, :]
                v.tensor_tensor(right, right, spread(block_products(par, g, m, 0), m), ALU.mult).then_inc(qd_ready, 1)

            def squares(c, which, g):
                dve.wait_ge((k_sq_ready, q_sq_ready)[which], c * G + g + 1)
                if not isinstance(c, int) or c or g or which:
                    dve.wait_ge(sq_sums_ready, c * 2 * G + 2 * g + which)
                link(v.transpose(sq_t[:, :], (k_sq, q_sq)[which][:, cols(g)]))
                n = W // Q
                ins = v.tensor_reduce(sq_sums[:, which, g * n:(g + 1) * n],
                                      sq_t[:, :].rearrange("p (n c) -> p n c", c=Q), AX, ALU.add)
                ins.then_inc(sq_sums_ready, 1)

            def take_norms(c, which):
                dve.wait_ge(norms_done, 2 * c + which + 1)
                v.tensor_scalar(sumsq[:, which * H:(which + 1) * H], bank_m[:, 256:256 + H], NORM_EPS ** 2, None,
                                ALU.max).then_inc(sumsq_ready, 1)

            def decay_products(c, par):
                dve.wait_ge(alpha_ready, (c + 1) * G)
                src, n = alphas[par][:, :], H * P
                for m in T_AT:
                    n //= 2
                    pair = src.rearrange("p (n two) -> p n two", two=2)
                    dst = t_prods[par][:, T_AT[m]:T_AT[m] + n]
                    ins = v.tensor_tensor(dst, pair[:, :, 0], pair[:, :, 1], ALU.mult)
                    if m == P:
                        ins.then_inc(t_ready, 1)
                    else:
                        link(ins)
                    src = dst

            def take_pair(i, par, pair):
                dve.wait_ge(level_done, pair_done(i, pair))
                by = "p (h t) -> p h t"
                src = bank_l[pair % 2][:, 0:2 * (P + P // 2)].rearrange(by, h=2)
                to = scoress[par][:, pair * 2 * P:(pair + 1) * 2 * P]
                hold(v.copy_predicated(to.rearrange(by, h=2), diag_sb[:, :].rearrange(by, h=2),
                                       src[:, :, 0:P])).then_inc(scores_ready, 1)
                dve.wait_ge(scores_ready, i * NEAR_READS + 2 * pair + 1)
                hold(v.copy_predicated(to.rearrange("p (h n two) -> p h n two", h=2, two=2)[:, :, :, 1],
                                       masks_sb[:, 0, 0:P].rearrange(by, h=2),
                                       src[:, :, P:P + P // 2])).then_inc(scores_ready, 1)

            def take_level(i, par, l, g):
                dve.wait_ge(level_done, step_done(i, l, g))
                query_update(par, g, l)
                if l < NEAR:
                    m = STEPS[l]
                    by = "p (n m) -> p n m"
                    hold(v.copy_predicated(halves(scoress[par], g, m)[:, :, 1, :],
                                           masks_sb[:, l, :].rearrange(by, m=m),
                                           bank_l[g][:, 0:W // 2].rearrange(by, m=m))).then_inc(scores_ready, 1)

            def take_outputs(c, par, g):
                dve.wait_ge(o_done, c * G + g + 1)
                dve.wait_ge(rnorm_ready, 2 * c + 2)
                if g == 0 and (not isinstance(c, int) or c):
                    dve.wait_ge(y_ready, c)
                by = "p (h d) -> p h d"
                v.tensor_tensor(o_sb[:, cols(g)].rearrange(by, h=HG), (bank_q, bank_a)[g][:, :].rearrange(by, h=HG),
                                spread(rq_norms[par][:, g * HG:(g + 1) * HG], P), ALU.mult).then_inc(o_ready, 1)

            def update_state(c, par, g):
                dve.wait_ge(update_done, c * G + g + 1)
                for h in range(g * HG, (g + 1) * HG):
                    s = state[:, bass.ds((c % B) * (H * P) + h * P, P)]
                    at = (h - g * HG) * P
                    last = v.scalar_tensor_tensor(s, s, t_prods[par][:, T_AT[P] + h:T_AT[P] + h + 1],
                                                  (bank_k, bank_q)[g][:, at:at + P], ALU.mult, ALU.add)
                last.then_inc(state_ready, 1)

            def residual(c, par):
                x1 = x1s[par]
                dve.wait_ge(y_ready, c + 1)
                link(v.tensor_tensor(y_gated[:, :].unsqueeze(1), y_sb[:, :].unsqueeze(1),
                                     gates[:, 0, bass.ds(c % B, 1), :], ALU.mult))
                dve.wait_ge(x_res_in, 16 * (c + 1))
                v.tensor_tensor(x1[:, :], y_gated[:, :], x_res[:, :], ALU.add).then_inc(x1_ready, 1)
                dve.wait_ge(x1_ready, c + 1)
                layer_norm_var(x1[:, :], 1)

            def choose(j):
                dve.wait_ge(gate_done, j + 1)
                link(v.tensor_tensor(gate_s[:, :], bank_m[:, 256:256 + E], gate_b_sb[:, :], ALU.add))
                link(v.tensor_reduce(gate_max[:, :], gate_s[:, :], AX, ALU.max))
                link(v.scalar_tensor_tensor(gate_rank[:, :], gate_s[:, :], gate_max[:, 0:1], desc_sb[:, :],
                                            ALU.is_equal, ALU.mult))
                link(v.tensor_reduce(gate_first[:, :], gate_rank[:, :], AX, ALU.max))
                ins = v.tensor_scalar(onehot[:, :], gate_rank[:, :], gate_first[:, 0:1], None, ALU.is_equal)
                ins.then_inc(onehot_ready, 1)

            def accumulate(j, e):
                dve.wait_ge(expert_done, j * E + e + 1)
                dve.wait_ge(acc_ready, j * (E + 1) + e + 1)
                v.scalar_tensor_tensor(acc[:, (e + 1) % 2, :], bank_y[:, 0:D], onehot[:, e:e + 1],
                                       acc[:, e % 2, :], ALU.mult, ALU.add).then_inc(acc_ready, 1)

            def finish(j, par):
                dve.wait_ge(acc_ready, (j + 1) * (E + 1))
                link(v.tensor_tensor(ffn_gated[:, :].unsqueeze(1), acc[:, E % 2, :].unsqueeze(1),
                                     gates[:, 1, bass.ds(j % B, 1), :], ALU.mult))
                dve.wait_ge(out_free, 16 * (j + 1))
                v.tensor_tensor(out_sb[:, :], ffn_gated[:, :], x1s[par][:, :], ALU.add).then_inc(out_ready, 1)

            def choice(j):
                dve.wait_ge(onehot_t_done, j + 1)
                v.tensor_copy(onehot_t[:, :], bank_m[0:E, 0:P]).then_inc(onehot_t_ready, 1)

            def bias(j):
                dve.wait_ge(bias_done, j + 1)
                v.tensor_copy(acc[:, 0, :], bank_m[:, 0:D]).then_inc(acc_ready, 1)

            def slot(i, par, parts):
                base[0], linked[0] = chain_start(i), 0
                other = 1 - par
                if NEXT in parts:
                    dve.wait_ge(x_next_in, 16 * (i + 3))
                    layer_norm_var(x_next[:, :], 0)
                for what, *n in ORDER:
                    if PART[what] not in parts:
                        continue
                    if what == "first":
                        take_pair(i, par, *n)
                    elif what == "level":
                        take_level(i, par, *n)
                    elif what == "a" and n[0]:
                        decay_products(i + 1, other)
                    elif what == "k":
                        squares(i + 1, 0, *n)
                    elif what == "q":
                        first_queries(i + 1, other, *n)
                        squares(i + 1, 1, *n)
                    elif what == "norms":
                        take_norms(i + 1, *n)
                    elif what == "values" and n[0] == 0:
                        dve.wait_ge(rstd_ready, i + 3)
                        layer_norm_scale(xn[:, :], x_next[:, :], 0, xn_ready)
                    elif what == "channels":
                        dve.wait_ge(xn_t_done, i + 3)
                        modulate(h_t[:, :], i + 2, CA, SA, h_t_ready)
                    elif what == "outputs":
                        take_outputs(i - 1, other, *n)
                    elif what == "updates":
                        update_state(i - 1, other, *n)
                    elif what == "channels2":
                        dve.wait_ge(xn2_t_done, i)
                        modulate(h2_ts[other][:, :], i - 1, CB, SB, h2_t_ready)
                    elif what == "gate":
                        choose(i - 1)
                    elif what == "choice":
                        choice(i - 2)
                    elif what == "bias":
                        bias(i - 2)
                    elif what == "expert":
                        accumulate(i - 2, *n)
                        if n[0] == E - 1:
                            finish(i - 2, par)
                    elif what == "residual":
                        residual(i - 1, other)
                    elif what == "norm2":
                        dve.wait_ge(rstd2_ready, i)
                        layer_norm_scale(xn2[:, :], x1s[other][:, :], 1, xn2_ready)
                assert linked[0] == sum(CHAINED[part] for part in parts)

            dve.wait_ge(weights_in, 16 * NW)
            dve.wait_ge(setup_act, 1)
            v.tensor_tensor(silu_c[:, :], silu_c[:, :], c_sb[:, :], ALU.mult).then_inc(setup_dve, 1)
            dve.wait_ge(setup_pe, 1)
            v.tensor_copy(c_t[:, :], bank_m[:, 0:B]).then_inc(setup_dve, 1)
            dve.wait_ge(setup_dve, 2)
            v.tensor_copy(c_wide[:, :, :], spread(c_t[:, :], P)).then_inc(setup_dve, 1)
            dve.wait_ge(setup_pe, 2)
            v.tensor_copy(mod_t[:, :, :].rearrange("p a b -> p (a b)"), bank_m[:, 64:64 + 6 * B]).then_inc(setup_dve, 1)
            dve.wait_ge(setup_dve, 4)
            for part in (CA, CB):
                v.tensor_scalar(mod_t[:, part, :], mod_t[:, part, :], 1.0, None, ALU.add).then_inc(setup_dve, 1)
            dve.wait_ge(setup_pe, 6)
            for n in range(2):
                for half in range(2):
                    src = (bank_a, bank_k, bank_q, bank_h)[2 * n + half][:, :].rearrange("p (b d) -> p b d", d=D)
                    sign = sq_t[:, :].rearrange("p (b d) -> p b d", d=D)
                    if 2 * n + half:
                        dve.wait_ge(setup_dve, 6 + 2 * n + half)
                    at = slice(half * (B // 2), (half + 1) * (B // 2))
                    g = gates[:, n, at, :]
                    link(v.tensor_scalar(sign, src, 0.0, 2.0, ALU.is_ge, ALU.mult))
                    link(v.scalar_tensor_tensor(g, sign, 1.0, src, ALU.subtract, ALU.mult))
                    link(v.tensor_scalar(g, g, GATE_FLOOR, None, ALU.max))
                    v.scalar_tensor_tensor(g, sign, 1.0, g, ALU.subtract, ALU.mult).then_inc(setup_dve, 1)
            dve.wait_ge(x_next_in, 16)
            layer_norm_var(x_next[:, :], 0)
            dve.wait_ge(rstd_ready, 1)
            dve.wait_ge(setup_dve, 10)
            v.memset(gate_first[:, :], 0.0).then_inc(setup_dve, 1)
            v.memset(out_sb[:, :], 0.0).then_inc(out_free, 16)
            dve.wait_ge(wv_t_done, 1)
            v.tensor_copy(o_sb[:, cols(0)], bank_a[:, :])
            v.tensor_copy(o_sb[:, cols(1)], bank_k[:, :]).then_inc(setup_dve, 1)
            dve.wait_ge(setup_pe, 7)
            v.tensor_copy(wvo_sb[:, cols(0)], bank_q[:, :])
            v.tensor_copy(wvo_sb[:, cols(1)], bank_h[:, :]).then_inc(setup_dve, 1)
            layer_norm_scale(xn[:, :], x_next[:, :], 0, xn_ready)
            dve.wait_ge(xn_t_done, 1)
            modulate(h_t[:, :], 0, CA, SA, h_t_ready)
            dve.wait_ge(setup_pool, 4)

            in_setup = linked[0]
            slots(dve, slot)


def kernel(**inputs):
    import numpy as np
    import concourse.bacc as bacc
    from concourse.bass_utils import run_bass_kernel_spmd

    a = {k: np.asarray(v) for k, v in inputs.items()}
    s = np.arange(P)[:, None]
    masks = []
    for m in STEPS[:NEAR]:
        t = np.array([t for t in range(P) if (t // m) % 2])[None, :]
        masks.append(np.tile((s // (2 * m) == t // (2 * m)) & ((s // m) % 2 == 0), (1, HG)))
    arrays = {
        "x": a["L0_attn_x"],
        "wq": a["L0_attn_Wq"], "wk": a["L0_attn_Wk"], "wv": a["L0_attn_Wv"], "wg": a["L0_attn_Wg"],
        "wo": a["L0_attn_Wo"].reshape(H, P, D).transpose(1, 0, 2).reshape(P, H * D),
        "gate_w": a["L0_ffn_Wg"],
        "gate_b": np.broadcast_to(a["L0_ffn_bg"], (P, E)),
        "w1": a["L0_ffn_W1"].transpose(1, 0, 2),
        "b1": a["L0_ffn_b1"].reshape(E * FC, P).transpose(1, 0),
        "w2": a["L0_ffn_W2"].reshape(E, FC, P, D).transpose(2, 0, 1, 3),
        "b2": a["L0_ffn_b2"],
        "c": a["L0_c"], "wmod": a["L0_wmod"],
        "ident": np.eye(P, dtype=np.float32),
        "fold": np.tile(np.eye(Q, dtype=np.float32), (P // Q, 1)),
        "level_masks": np.concatenate(masks, axis=1).astype(np.int32),
        "diag_mask": np.tile(np.eye(P, dtype=np.int32), (1, 2)),
        "descending": np.broadcast_to(np.arange(E, 0, -1, dtype=np.float32), (P, E)),
    }
    nc = bacc.Bacc("TRN2", target_bir_lowering=False, num_devices=1)
    arrays = {k: np.ascontiguousarray(v) for k, v in arrays.items()}
    args = [nc.dram_tensor(k, v.shape, mybir.dt.from_np(v.dtype), kind="ExternalInput").ap()
            for k, v in arrays.items()]
    out = nc.dram_tensor("out", (B, T, D), F32, kind="ExternalOutput").ap()
    adaln_gla_moe(nc, *args, out)
    r = run_bass_kernel_spmd(nc, [arrays], core_ids=[0])
    return r.results[0]["out"]
```

```python
from contextlib import ExitStack

import concourse.bass as bass
from concourse import mybir

F32 = mybir.dt.float32
I32 = mybir.dt.int32
ALU = mybir.AluOpType
ACT = mybir.ActivationFunctionType
AX = mybir.AxisListType.X

P = 128
B, T, D = 8, 1024, 128
H = 8
E, F = 8, 512
FC = F // P
NCHUNK = B * T // P
STEPS = [1, 2, 4, 8, 16, 32, 64]
NS = len(STEPS)
NEAR = 5
G = 2
HG = H // G
W = HG * P
LN_EPS = 1e-5
NORM_EPS = 1e-12
GATE_FLOOR = 0.25
SA, CA, GA, SB, CB, GB = range(6)
T_AT = {}
for _m in (2, 4, 8, 16, 32, 64, 128):
    T_AT[_m] = sum(H * P // n for n in T_AT)
T_LEN = sum(H * P // n for n in T_AT)

ORDER = [
    ("first", 0), ("first", 1), ("a", 0), ("first", 2), ("keys_tok", 0), ("first", 3), ("gate",), ("keys_tok", 1),
    ("level", 1, 0), ("k", 0), ("outputs", 0), ("norm1",), ("level", 1, 1), ("a", 1), ("rstd1",), ("outputs", 1),
    ("level", 2, 0), ("updates", 0), ("scale1",), ("route",), ("level", 2, 1), ("updates", 1), ("channels",), ("q", 0),
    ("level", 3, 0), ("k", 1), ("norms", 0, 0), ("heads", 0), ("level", 3, 1), ("q", 1), ("norms", 1, 0),
    ("heads", 1), ("level", 4, 0), ("norms", 0, 1), ("decays", 0), ("heads", 2), ("level", 4, 1), ("norms", 1, 1),
    ("sumsq",), ("residual",), ("level", 5, 0), ("decays", 1), ("rnorm", 0), ("level", 5, 1), ("rstd2",),
    ("values", 0), ("level", 6, 0), ("norm2",), ("values", 1), ("level", 6, 1), ("channels2",), ("rnorm", 1),
]
OWN, TAIL, NEXT, ROUTE = "own", "tail", "next", "route"
PART = {"first": OWN, "level": OWN, "keys_tok": TAIL, "outputs": TAIL, "updates": TAIL, "channels2": TAIL,
        "heads": TAIL, "residual": TAIL, "rstd2": TAIL, "norm2": TAIL, "decays": NEXT, "norm1": NEXT,
        "rstd1": NEXT, "rnorm": NEXT, "scale1": NEXT, "sumsq": NEXT,
        "gate": ROUTE, "a": NEXT, "k": NEXT, "q": NEXT, "values": NEXT, "norms": NEXT, "channels": NEXT,
        "route": ROUTE}
ALL = (OWN, TAIL, NEXT, ROUTE)
CHAINED = {OWN: 0, TAIL: 4, NEXT: 8, ROUTE: 7}
PROLOGUE = [(-1, (NEXT,)), (0, (OWN, NEXT)), (1, (OWN, TAIL, NEXT))]
EPILOGUE = [(NCHUNK, (TAIL, ROUTE)), (NCHUNK + 1, (ROUTE,))]
SUM_COLS = 512 // (2 * H)
TILES = NCHUNK + E
AHEAD = 3
RING = 8
SLOT_ROWS = TILES
TABLE_ROWS = E * SLOT_ROWS + AHEAD
EXPERT_W = F + FC


def adaln_gla_moe(nc, x, wq, wk, wv, wg, wo, gate_w, gate_b, w1, w2, b2, c, wmod,
                  ident, level_masks, diag_mask, descending, before, earlier, thresholds, region, tile_no,
                  row_numbers, spare_numbers, rows, slots_table, out):
    with ExitStack() as ctx:
        def sb(name, shape, dt=F32):
            return ctx.enter_context(nc.sbuf_tensor(name, shape, dt))

        def bank(name):
            return ctx.enter_context(nc.psum_tensor(name, [P, 512], F32))

        def sem(name):
            return ctx.enter_context(nc.semaphore(name))

        wq_sb, wk_sb, wvo_sb, wg_sb = (sb(f"w{n}_sb", [P, H * P]) for n in ("q", "k", "vo", "g"))
        w1_sb = sb("w1_sb", [P, E * EXPERT_W])
        w2_sb = sb("w2_sb", [P, E * FC * D])
        b2_sb = sb("b2_sb", [1, E * D])
        gate_w_sb = sb("gate_w_sb", [P, E])
        gate_b_sb = sb("gate_b_sb", [P, E])
        ident_sb = sb("ident_sb", [P, P])
        masks_sb = sb("masks_sb", [P, NEAR, W // 2], I32)
        diag_sb = sb("diag_sb", [P, 2 * P], I32)
        desc_sb = sb("desc_sb", [P, E])
        minus_half = sb("minus_half", [P, H])
        c_sb = sb("c_sb", [B, P])
        silu_c = sb("silu_c", [B, P])
        c_t = sb("c_t", [P, B])
        c_wide = sb("c_wide", [P, B, P])
        wmod_sb = sb("wmod_sb", [P, 6, D])
        mod_t = sb("mod_t", [P, 6, B])
        mod_rows = sb("mod_rows", [P, 4, B, D])
        state = sb("state", [P, B * H * P])
        def twice(name, shape):
            return [sb(f"{name}{n}", shape) for n in range(2)]

        alphas, qds, kds, scoress, vs = (twice(n, [P, H * P]) for n in ("alpha", "qd", "kd", "scores", "v"))
        t_prods = twice("t_prod", [P, T_LEN])
        h2_x1s = twice("h2_x1_", [P, 2, D])
        rq_norms = twice("rq_norm", [P, H])
        rk_norm = sb("rk_norm", [P, H])
        x_next = sb("x_next", [P, D])
        x_res = sb("x_res", [P, D])
        stats = sb("stats", [P, 2, 6])
        mean_var = sb("mean_var", [P, 2, 2])
        var_eps = sb("var_eps", [P, 2])
        rstd = sb("rstd", [P, 2])
        xn = sb("xn", [P, D])
        scaled2 = sb("scaled2", [P, D])
        h2_t = sb("h2_t", [P, P])
        h_ts = twice("h_t", [P, P])
        q_first = sb("q_first", [P, H, P + P // 2])
        q_sq = sb("q_sq", [P, H * P])
        k_sq = sb("k_sq", [P, H * P])
        k_tok = sb("k_tok", [P, H * P])
        o_sb = sb("o_sb", [P, H * P])
        o_pairs = sb("o_pairs", [P, 6 * D])
        y_sb = sb("y_sb", [P, D])
        sign_sb = sb("sign_sb", [P, W])
        sumsq = sb("sumsq", [P, 2 * H])
        y_gated = sb("y_gated", [P, D])
        gate_s = sb("gate_s", [P, E])
        gate_max = sb("gate_max", [P, 1])
        gate_rank = sb("gate_rank", [P, E])
        gate_first = sb("gate_first", [P, 1])
        onehot = sb("onehot", [P, E])
        before_sb = sb("before_sb", [P, P])
        ones_sb = sb("ones_sb", [P, P])
        earlier_sb = sb("earlier_sb", [P, E, E])
        thresholds_sb = sb("thresholds_sb", [P, NCHUNK])
        region_sb = sb("region_sb", [P, E])
        tile_no_sb = sb("tile_no_sb", [P, 1])
        row_numbers_sb = sb("row_numbers_sb", [P, NCHUNK])
        spare_sb = sb("spare_sb", [P, TABLE_ROWS])
        next_free = sb("next_free", [P, E])
        free_by_expert = sb("free_by_expert", [P, E])
        own_slot = sb("own_slot", [P, E])
        slot_number = sb("slot_number", [P, 1])
        slot_no = sb("slot_no", [P, 1], I32)
        chunk_rows = sb("chunk_rows", [P, 1])
        counts = sb("counts", [P, E])
        started = sb("started", [P, E, NCHUNK])
        expert_tiles = sb("expert_tiles", [P, E])
        tiles_earlier = sb("tiles_earlier", [P, E, E])
        tiles_to = sb("tiles_to", [P, E])
        passed = sb("passed", [P, E - 1])
        tile_expert = sb("tile_expert", [P, 1])
        tiles_passed = sb("tiles_passed", [P, E - 1])
        first_tile = sb("first_tile", [P, 1])
        tile_within = sb("tile_within", [P, 1])
        table_row = sb("table_row", [P, 1], I32)
        expert_row = sb("expert_row", [1, P], I32)
        tile_slots = sb("tile_slots", [TILES + AHEAD, P])
        token_rows = sb("token_rows", [P, TILES + AHEAD], I32)
        token_row = [sb(f"token_row{n}", [P, 1], I32) for n in range(RING)]
        ring = [buf[:, at:at + 4 * D] for buf in (*alphas, *qds) for at in (0, 4 * D)]
        tile_w1 = [buf[:, 0:EXPERT_W] for buf in kds]
        tile_h, gated = ([o_sb[:, at + n * P:at + (n + 1) * P] for n in range(2)] for at in (0, 2 * P))
        hid = [q_sq[:, n * F:(n + 1) * F].rearrange("p (f t) -> p f t", f=FC) for n in range(2)]

        bank_a = bank("bank_a")
        bank_k = bank("bank_k")
        bank_q = bank("bank_q")
        bank_l = [bank("bank_l0"), bank("bank_l1")]
        bank_m = bank("bank_m")
        bank_h = bank("bank_h")
        bank_y = bank("bank_y")
        bank_tail = (bank_h, bank_y)
        bank_t, bank_hid, bank_out = (bank_m, bank_q), (bank_h, bank_a), (bank_y, bank_k)

        weights_in = sem("weights_in")
        expert_weights_in = sem("expert_weights_in")
        x_next_in = sem("x_next_in")
        x_res_in = sem("x_res_in")
        table_cleared = sem("table_cleared")
        rows_stored = sem("rows_stored")
        slots_stored = sem("slots_stored")
        tile_slots_in = sem("tile_slots_in")
        tile_in, tile_stored = ([sem(f"{name}{n}") for n in range(RING)] for name in ("tile_in", "tile_stored"))
        setup_dve = sem("setup_dve")
        setup_pe = sem("setup_pe")
        setup_act = sem("setup_act")
        setup_pool = sem("setup_pool")
        a_done, k_done, q_done, v_done = (sem(f"{n}_done") for n in "akqv")
        norms_done = sem("norms_done")
        level_done = sem("level_done")
        wv_t_done = sem("wv_t_done")
        k_tok_done = sem("k_tok_done")
        o_done = sem("o_done")
        update_done = sem("update_done")
        xn_t_done = sem("xn_t_done")
        h2_t_done = sem("h2_t_done")
        gate_done = sem("gate_done")
        ranks_done = sem("ranks_done")
        plan_done = sem("plan_done")
        tile_t_done, tile_hid_done, tile_y_done = (sem(f"tile_{n}_done") for n in ("t", "hid", "y"))
        alpha_ready = sem("alpha_ready")
        kd_first = sem("kd_first")
        k_sq_ready = sem("k_sq_ready")
        q_raw_ready = sem("q_raw_ready")
        q_sq_ready = sem("q_sq_ready")
        v_ready = sem("v_ready")
        k_tok_ready = sem("k_tok_ready")
        far_ready = sem("far_ready")
        y_ready = sem("y_ready")
        pool_step = sem("pool_step")
        q_first_ready = sem("q_first_ready")
        qd_ready = sem("qd_ready")
        kd_ready = sem("kd_ready")
        t_ready = sem("t_ready")
        scores_ready = sem("scores_ready")
        sumsq_ready = sem("sumsq_ready")
        rnorm_ready = sem("rnorm_ready")
        var_ready, var2_ready = sem("var_ready"), sem("var2_ready")
        rstd_ready, rstd2_ready = sem("rstd_ready"), sem("rstd2_ready")
        xn_ready = sem("xn_ready")
        h2_ready = sem("h2_ready")
        h_t_ready = sem("h_t_ready")
        h2_t_ready = sem("h2_t_ready")
        onehot_ready = sem("onehot_ready")
        ranks_taken = sem("ranks_taken")
        slot_ready = sem("slot_ready")
        plan_ready = sem("plan_ready")
        expert_row_ready = sem("expert_row_ready")
        token_rows_ready = sem("token_rows_ready")
        token_row_ready = sem("token_row_ready")
        tile_w1_ready, tile_h_ready, tile_hid_ready, gated_ready, tile_out_ready = (
            sem(f"{n}_ready") for n in ("tile_w1", "tile_h", "tile_hid", "gated", "tile_out"))
        o_ready = sem("o_ready")
        state_ready = sem("state_ready")
        x1_ready = sem("x1_ready")
        dve_step = sem("dve_step")

        LEVELS_DONE = 2 * G + (NS - 1) * G
        NEAR_READS = (4 + NEAR - 1) * G
        NW = 21

        def x_rows(tensor, i):
            return tensor[bass.ds(i % B, 1), bass.ds((i // B) * P, P), :].rearrange("a t d -> (a t) d")

        def cols(g):
            return slice(g * W, (g + 1) * W)

        def head(buf, h):
            return buf[:, h * P:(h + 1) * P]

        def q_first_signal(i, l, g):
            return i * (2 * G) + 2 * g + l + 1

        def q_signal(i, l, g):
            return (i * (NS - 1) + l - 2) * G + g + 1

        def k_signal(i, l, g):
            return (i * NS + l - 1) * G + g + 1

        def pair_done(i, pair):
            return i * LEVELS_DONE + pair + 1

        def step_done(i, l, g):
            return i * LEVELS_DONE + 2 * G + (l - 1) * G + g + 1

        def near_read(i, l, g):
            at = 2 * (G + g + 1) if l == 0 else 4 * G + (l - 1) * G + g + 1
            return i * NEAR_READS + at

        def far_read(i, l, g):
            return (i * (NS - NEAR) + l - NEAR) * G + g + 1

        def halves(buf, g, m):
            return buf[:, cols(g)].rearrange("p (n two m) -> p n two m", two=2, m=m)

        def block_products(par, g, m, side):
            n = W // m
            buf = alphas[par][:, cols(g)] if m == 1 else t_prods[par][:, T_AT[m] + g * n:T_AT[m] + (g + 1) * n]
            return buf.rearrange("p (n two) -> p n two", two=2)[:, :, side]

        def slots(engine, slot):
            for i, parts in PROLOGUE:
                slot(i, i % 2, parts)
            with engine.Fori(1, NCHUNK // 2) as n:
                for par in range(2):
                    slot(n * 2 + par, par, ALL)
            for i, parts in EPILOGUE:
                slot(i, i % 2, parts)

        def hold(ins):
            return ins.wait_op(weights_in, 16 * NW, "sem-ge")

        def tiles(engine, step):
            for n in range(RING):
                step(n, n)
            with engine.Fori(1, TILES // RING) as turn:
                for r in range(RING):
                    step(turn * RING + r, r)
            for n in (TILES, TILES + 1):
                step(n, n % RING)

        def turns(n):
            return (n // RING + 1) * 16

        def live(n):
            return not isinstance(n, int) or 0 <= n < TILES

        def third(n):
            return not isinstance(n, int) or n >= 2

        def spread(ap, m):
            return ap.unsqueeze(2).broadcast_to((P, ap.shape[1], m))

        block = ctx.enter_context(nc.Block())

        @block.sync
        def _(sp):
            loads = [(c_sb[:, :], c), (wmod_sb[:, :, :].rearrange("p a b -> p (a b)"), wmod),
                     (ident_sb[:, :], ident), (wg_sb[:, :], wg), (wk_sb[:, :], wk), (wq_sb[:, :], wq),
                     (vs[0][:, :], wv), (k_tok[:, :], wo),
                     (masks_sb[:, :, :].rearrange("p a b -> p (a b)"), level_masks),
                     (diag_sb[:, :], diag_mask), (gate_w_sb[:, :], gate_w),
                     (gate_b_sb[:, :], gate_b), (desc_sb[:, :], descending), (b2_sb[:, :], b2),
                     (before_sb[:, :], before), (earlier_sb[:, :, :].rearrange("p a b -> p (a b)"), earlier),
                     (thresholds_sb[:, :], thresholds), (region_sb[:, :], region), (tile_no_sb[:, :], tile_no),
                     (row_numbers_sb[:, :], row_numbers), (spare_sb[:, :], spare_numbers)]
            sp.dma_start(x_next[:, :], x_rows(x, 0)).then_inc(x_next_in, 16)
            sp.dma_start(x_res[:, :], x_rows(x, 0)).then_inc(x_res_in, 16)
            for to, of in loads:
                sp.dma_start(to, of).then_inc(weights_in, 16)
            for e in range(0, E, 4):
                at, w2_at = slice(e * EXPERT_W, (e + 4) * EXPERT_W), slice(e * FC * D, (e + 4) * FC * D)
                sp.dma_start(w1_sb[:, at], w1[:, at]).then_inc(expert_weights_in, 16)
                sp.dma_start(w2_sb[:, w2_at], w2[:, w2_at]).then_inc(expert_weights_in, 16)

            def slot(i, par, parts):
                if NEXT in parts:
                    sp.wait_ge(xn_ready, i + 3)
                    sp.dma_start(x_next[:, :], x_rows(x, (i + 3) % NCHUNK)).then_inc(x_next_in, 16)
                if TAIL in parts:
                    sp.wait_ge(x1_ready, i)
                    sp.dma_start(x_res[:, :], x_rows(x, i % NCHUNK)).then_inc(x_res_in, 16)
                if TAIL in parts:
                    sp.wait_ge(h2_ready, i)
                    to = rows[bass.ds(((i - 1) % B) * T + ((i - 1) // B) * P, P), :]
                    h2_x1 = h2_x1s[1 - par][:, :, :].rearrange("p a d -> p (a d)")
                    gb = mod_rows[:, 1, bass.ds((i - 1) % B, 1), :].rearrange("p a d -> p (a d)")
                    sp.dma_start(to[:, 0:2 * D], h2_x1).then_inc(rows_stored, 16)
                    sp.dma_start(to[:, 2 * D:3 * D], gb).then_inc(rows_stored, 16)

            sp.wait_ge(weights_in, 16 * NW)
            all_slots = slots_table[:, :].rearrange("r p -> (r p)").rearrange("(a b) -> a b", a=P)
            sp.dma_start(all_slots, spare_sb[:, :]).then_inc(table_cleared, 16)
            sp.dma_start(rows[B * T:B * T + P, :], wq_sb[:, 0:3 * D]).then_inc(table_cleared, 16)
            sp.wait_ge(xn_ready, 1)
            sp.dma_start(x_next[:, :], x_rows(x, 1)).then_inc(x_next_in, 16)
            slots(sp, slot)
            sp.wait_ge(x_next_in, 16 * (NCHUNK + 3))
            sp.wait_ge(x_res_in, 16 * (NCHUNK + 1))
            sp.wait_ge(table_cleared, 32)
            sp.wait_ge(rows_stored, 32 * NCHUNK)

        @block.tensor
        def _(pe):
            mm = nc.tensor.matmul

            def transpose_input(c):
                pe.wait_ge(xn_ready, c + 1)
                nc.tensor.transpose(bank_m[:, 0:P], xn[:, :], ident_sb[:, :]).then_inc(xn_t_done, 1)

            def project(g, w, par, to, done):
                for h in range(HG):
                    last = mm(to[:, h * P:(h + 1) * P], head(w, g * HG + h), h_ts[par][:, :], start=True, stop=True)
                last.then_inc(done, 1)

            def projection(c, par, which, g):
                if which == "a":
                    if g:
                        pe.wait_ge(alpha_ready, c * G + 1)
                    else:
                        pe.wait_ge(h_t_ready, c + 1)
                        if not isinstance(c, int) or c:
                            pe.wait_ge(v_ready, c * G)
                    project(g, wg_sb, par, bank_a, a_done)
                elif which == "k":
                    if g:
                        pe.wait_ge(k_sq_ready, c * G + 1)
                    elif not isinstance(c, int) or c:
                        pe.wait_ge(v_ready, c * G)
                    project(g, wk_sb, par, bank_k, k_done)
                else:
                    if not isinstance(c, int) or c or g:
                        pe.wait_ge(q_sq_ready, c * G + g)
                    project(g, wq_sb, par, bank_q, q_done)

            def norms(c, which, g):
                pe.wait_ge((k_sq_ready, q_sq_ready)[which], c * G + g + 1)
                if which == 0 and g == 0:
                    pe.wait_ge(h_t_ready, c + 2)
                for h in range(g * HG, (g + 1) * HG):
                    at = (which * H + h) * SUM_COLS
                    last = mm(bank_m[:, at:at + SUM_COLS], head((k_sq, q_sq)[which], h), ones_sb[:, 0:SUM_COLS],
                              start=True, stop=True)
                last.then_inc(norms_done, 1)

            def first(i, par, pair):
                g = pair // 2
                to = bank_l[pair % 2]
                if pair >= 2:
                    pe.wait_ge(scores_ready, i * NEAR_READS + 2 * (pair - 1))
                elif not isinstance(i, int) or i:
                    pe.wait_ge(far_ready, far_read(i - 1, NS - 1, pair))
                pe.wait_ge(k_sq_ready, i * G + g + 1)
                pe.wait_ge(q_first_ready, q_first_signal(i, 0, g))
                for n in range(2):
                    h = pair * 2 + n
                    at = n * (P + P // 2)
                    last = mm(to[:, at:at + P + P // 2], head(kds[par], h), q_first[:, h, :], start=True, stop=True)
                last.then_inc(level_done, 1)

            def level(i, par, l, g):
                m = STEPS[l]
                if l == 1:
                    pe.wait_ge(q_first_ready, q_first_signal(i, l, g))
                else:
                    pe.wait_ge(qd_ready, q_signal(i, l, g))
                pe.wait_ge(kd_ready, k_signal(i, l, g))
                if l <= NEAR:
                    pe.wait_ge(scores_ready, near_read(i, l - 1, g))
                else:
                    pe.wait_ge(far_ready, far_read(i, l - 1, g))
                for h in range(g * HG, (g + 1) * HG):
                    k, q, n = head(kds[par], h), head(qds[par], h), h - g * HG
                    if l < NEAR:
                        rhs = q.rearrange("p (n two m) -> p n two m", two=2, m=m)[:, :, 1, :]
                        last = mm(bank_l[g][:, n * P // 2:(n + 1) * P // 2], k, rhs, start=True, stop=True)
                    else:
                        for at in range(0, P, 2 * m):
                            last = mm(bank_l[g][at:at + m, n * m:(n + 1) * m], k[:, at:at + m],
                                      q[:, at + m:at + 2 * m], start=True, stop=True)
                last.then_inc(level_done, 1)

            def values(c, par, g):
                if g == 0:
                    pe.wait_ge(alpha_ready, (c + 1) * G)
                else:
                    pe.wait_ge(k_sq_ready, (c + 1) * G)
                mm((bank_a, bank_k)[g][:, :], h_ts[par][:, :], wvo_sb[:, cols(g)], start=True, stop=True).then_inc(v_done, 1)

            def keys_tok(c, par, g):
                pe.wait_ge(kd_ready, k_signal(c, NS, g))
                if not isinstance(c, int) or c:
                    pe.wait_ge(state_ready, (c - 1) * G + g + 1)
                for h in range(HG):
                    last = nc.tensor.transpose(bank_tail[g][:, h * P:(h + 1) * P], head(kds[par], g * HG + h),
                                               ident_sb[:, :])
                last.then_inc(k_tok_done, 1)

            def outputs(c, par, g):
                pe.wait_ge(qd_ready, q_signal(c, NS, g))
                pe.wait_ge(scores_ready, near_read(c, NEAR - 1, g))
                pe.wait_ge(far_ready, far_read(c, NS - 1, g))
                if not isinstance(c, int) or c:
                    pe.wait_ge(state_ready, c * G)
                pe.wait_ge(k_tok_ready, c * G + g + 1)
                to = bank_tail[g]
                base = (c % B) * (H * P)
                for h in range(g * HG, (g + 1) * HG):
                    at = (h - g * HG) * P
                    mm(to[:, at:at + P], head(qds[par], h), state[:, bass.ds(base + h * P, P)],
                       start=True, stop=False)
                    last = mm(to[:, at:at + P], head(scoress[par], h), head(vs[par], h), start=False, stop=True)
                last.then_inc(o_done, 1)

            def updates(c, par, g):
                pe.wait_ge(k_tok_ready, c * G + g + 1)
                pe.wait_ge(o_ready, c * G + g + 1)
                for h in range(HG):
                    last = mm(bank_tail[g][:, h * P:(h + 1) * P], head(k_tok, g * HG + h),
                              head(vs[par], g * HG + h), start=True, stop=True)
                last.then_inc(update_done, 1)

            def channels2(c, par, nxt):
                if nxt:
                    pe.wait_ge(sumsq_ready, c + 3)
                else:
                    pe.wait_ge(ranks_taken, c)
                pe.wait_ge(h2_ready, c + 1)
                nc.tensor.transpose(bank_m[:, 0:P], h2_x1s[par][:, 0, :], ident_sb[:, :]).then_inc(h2_t_done, 1)

            def channels(c, routed):
                if routed:
                    pe.wait_ge(ranks_taken, c - 3)
                elif c >= 2:
                    pe.wait_ge(sumsq_ready, c - 1)
                transpose_input(c)

            def gate(c):
                pe.wait_ge(h2_t_ready, c + 1)
                mm(bank_m[:, 256:256 + E], h2_t[:, :], gate_w_sb[:, :], start=True, stop=True).then_inc(gate_done, 1)

            def route(j):
                pe.wait_ge(onehot_ready, j + 1)
                mm(bank_m[:, 0:E], before_sb[:, :], onehot[:, :], start=True, stop=True)
                mm(bank_m[:, E:2 * E], ones_sb[:, :], onehot[:, :], start=True, stop=True).then_inc(ranks_done, 1)

            def slot(i, par, parts):
                nxt = NEXT in parts
                for what, *n in ORDER:
                    if PART[what] not in parts:
                        continue
                    if what == "first":
                        first(i, par, *n)
                    elif what == "level":
                        level(i, par, *n)
                    elif what in ("a", "k", "q"):
                        projection(i + 1, 1 - par, what, n[0])
                    elif what == "norms":
                        norms(i + 1, *n)
                    elif what == "values":
                        values(i + 1, 1 - par, *n)
                    elif what == "channels":
                        channels(i + 2, ROUTE in parts)
                    elif what == "keys_tok":
                        keys_tok(i - 1, 1 - par, *n)
                    elif what == "outputs":
                        outputs(i - 1, 1 - par, *n)
                    elif what == "updates":
                        updates(i - 1, 1 - par, *n)
                    elif what == "channels2":
                        channels2(i - 1, 1 - par, nxt)
                    elif what == "gate":
                        gate(i - 2)
                    elif what == "route":
                        route(i - 2)

            def tile_step(n, r):
                if live(n):
                    pe.wait_ge(tile_in[r], turns(n))
                    if third(n):
                        pe.wait_ge(tile_h_ready, n - 1)
                    nc.tensor.transpose(bank_t[r % 2][:, 0:P], ring[r][:, 0:D], ident_sb[:, :]).then_inc(tile_t_done, 1)
                if live(n - 1):
                    b = (r - 1) % 2
                    pe.wait_ge(tile_w1_ready, n)
                    pe.wait_ge(tile_h_ready, n)
                    if third(n - 1):
                        pe.wait_ge(tile_hid_ready, n - 2)
                    for f in range(FC):
                        last = mm(bank_hid[b][:, f * P:(f + 1) * P], tile_w1[b][:, f * P:(f + 1) * P], tile_h[b][:, :],
                                  start=True, stop=True)
                    last.then_inc(tile_hid_done, 1)
                if live(n - 2):
                    expert = pe.value_load(expert_row[0:1, bass.ds(n - 2, 1)], min_val=0, max_val=E - 1)
                    pe.wait_ge(tile_hid_ready, n - 1)
                    if third(n - 2):
                        pe.wait_ge(gated_ready, n - 3)
                    to = bank_out[r % 2][:, 0:D]
                    for f in range(FC):
                        mm(to, hid[r % 2][:, f, :], w2_sb[:, bass.ds(expert * (FC * D) + f * D, D)],
                           start=(f == 0), stop=False)
                    mm(to, ones_sb[0:1, :], b2_sb[:, bass.ds(expert * D, D)], start=False,
                       stop=True).then_inc(tile_y_done, 1)

            pe.wait_ge(weights_in, 16 * NW)
            pe.wait_ge(setup_dve, 1)
            nc.tensor.transpose(bank_m[:, 0:B], silu_c[:, :], ident_sb[0:B, 0:B]).then_inc(setup_pe, 1)
            pe.wait_ge(setup_dve, 3)
            for n in range(6):
                last = mm(bank_m[:, 64 + n * B:64 + (n + 1) * B], wmod_sb[:, n, :], c_t[:, :], start=True, stop=True)
            last.then_inc(setup_pe, 1)
            pe.wait_ge(setup_dve, 4)
            pe.wait_ge(setup_pool, 5)
            for n, part in enumerate((GA, GB, CB, SB)):
                for half in range(2):
                    to = (bank_a, bank_k, bank_q, bank_h, *bank_l, bank_y, bank_m)[2 * n + half]
                    for b in range(B // 2):
                        last = mm(to[:, b * D:(b + 1) * D], c_wide[:, half * (B // 2) + b, :], wmod_sb[:, part, :],
                                  start=True, stop=True)
                    last.then_inc(setup_pe, 1)
            pe.wait_ge(setup_dve, 13)
            for h in range(H):
                to = (bank_a, bank_k)[h // HG]
                at = h % HG * P
                last = nc.tensor.transpose(to[:, at:at + P], head(vs[0], h), ident_sb[:, :])
            last.then_inc(wv_t_done, 1)
            pe.wait_ge(setup_dve, 15)
            for h in range(H):
                to = (bank_q, bank_h)[h // HG]
                at = h % HG * P
                last = mm(to[:, at:at + P], head(o_sb, h), head(k_tok, h), start=True, stop=True)
            last.then_inc(setup_pe, 1)
            transpose_input(0)
            pe.wait_ge(setup_dve, 16)
            slots(pe, slot)
            pe.wait_ge(plan_ready, 1)
            pe.wait_ge(ranks_taken, NCHUNK)
            mm(bank_m[0:1, 0:P], tile_expert[:, 0:1], ident_sb[:, :], start=True, stop=True).then_inc(plan_done, 1)
            pe.wait_ge(expert_row_ready, 1)
            pe.wait_ge(tile_slots_in, 16)
            n = TILES + AHEAD
            nc.tensor.transpose(bank_m[:, 0:n], tile_slots[:, :], ident_sb[0:n, 0:n]).then_inc(plan_done, 1)
            pe.wait_ge(token_rows_ready, 1)
            pe.wait_ge(v_ready, (NCHUNK + 1) * G)
            pe.wait_ge(q_sq_ready, (NCHUNK + 1) * G)
            pe.wait_ge(state_ready, NCHUNK * G)
            pe.wait_ge(o_ready, NCHUNK * G)
            pe.wait_ge(expert_weights_in, 64)
            tiles(pe, tile_step)

        @block.scalar
        def _(act):
            def fn(out_, in_, what, **kw):
                return nc.scalar.activation(out_, in_, what, **kw)

            def projection(c, par, which, g):
                hs = slice(g * HG, (g + 1) * HG)
                if which == "a":
                    act.wait_ge(a_done, c * G + g + 1)
                    fn(alphas[par][:, cols(g)], bank_a[:, :], ACT.Sigmoid).then_inc(alpha_ready, 1)
                elif which == "k":
                    act.wait_ge(k_done, c * G + g + 1)
                    fn(kds[par][:, cols(g)], bank_k[:, :], ACT.Copy)
                    fn(k_sq[:, cols(g)], bank_k[:, :], ACT.Square).then_inc(k_sq_ready, 1)
                else:
                    act.wait_ge(q_done, c * G + g + 1)
                    fn(q_first[:, hs, 0:P], bank_q[:, :].rearrange("p (h t) -> p h t", h=HG),
                       ACT.Copy).then_inc(q_raw_ready, 1)
                    fn(q_sq[:, cols(g)], bank_q[:, :], ACT.Square).then_inc(q_sq_ready, 1)

            def values(c, par, g):
                act.wait_ge(v_done, c * G + g + 1)
                act.wait_ge(rnorm_ready, 2 * c + 1)
                src = (bank_a, bank_k)[g]
                for h in range(HG):
                    n = g * HG + h
                    last = fn(head(vs[par], n), src[:, h * P:(h + 1) * P], ACT.Copy, scale=rk_norm[:, n:n + 1])
                last.then_inc(v_ready, 1)

            def far_scores(i, par, l, g):
                m = STEPS[l]
                act.wait_ge(level_done, step_done(i, l, g))
                to = scoress[par][:, cols(g)].rearrange("p (h t) -> p h t", h=HG)
                for at in range(0, P, 2 * m):
                    last = fn(to[at:at + m, :, at + m:at + 2 * m],
                              bank_l[g][at:at + m, 0:HG * m].rearrange("p (h t) -> p h t", h=HG), ACT.Copy)
                last.then_inc(far_ready, 1)

            def keys_tok(c, g):
                act.wait_ge(k_tok_done, c * G + g + 1)
                fn(k_tok[:, cols(g)], bank_tail[g][:, :], ACT.Copy).then_inc(k_tok_ready, 1)

            def slot(i, par, parts):
                for what, *n in ORDER:
                    if PART[what] not in parts:
                        continue
                    if what == "level" and n[0] >= NEAR:
                        far_scores(i, par, *n)
                    elif what in ("a", "k", "q"):
                        projection(i + 1, 1 - par, what, *n)
                    elif what == "values":
                        values(i + 1, 1 - par, *n)
                    elif what == "keys_tok":
                        keys_tok(i - 1, *n)

            def tile_step(n, r):
                if live(n):
                    expert = act.value_load(expert_row[0:1, bass.ds(n, 1)], min_val=0, max_val=E - 1)
                    if third(n):
                        act.wait_ge(tile_hid_done, n - 1)
                        act.wait_ge(tile_hid_ready, n - 1)
                    hold(fn(tile_w1[r % 2][:, :], w1_sb[:, bass.ds(expert * EXPERT_W, EXPERT_W)],
                            ACT.Copy)).then_inc(tile_w1_ready, 1)
                if live(n - 1):
                    b = (r - 1) % 2
                    act.wait_ge(tile_w1_ready, n)
                    act.wait_ge(tile_hid_done, n)
                    if third(n - 1):
                        act.wait_ge(tile_y_done, n - 2)
                    for f in range(FC):
                        last = fn(hid[b][:, f, :], bank_hid[b][:, f * P:(f + 1) * P], ACT.Relu,
                                  bias=tile_w1[b][:, F + f:F + f + 1])
                    last.then_inc(tile_hid_ready, 1)

            act.wait_ge(weights_in, 16 * NW)
            fn(silu_c[:, :], c_sb[:, :], ACT.Sigmoid).then_inc(setup_act, 1)
            slots(act, slot)
            act.wait_ge(expert_row_ready, 1)
            act.wait_ge(expert_weights_in, 64)
            tiles(act, tile_step)

        @block.gpsimd
        def _(pool):
            def rsqrt(out_, in_):
                return nc.gpsimd.tensor_tensor(out_, in_, minus_half[:, 0:in_.shape[1]], ALU.pow)

            def norm(c, par, which):
                pool.wait_ge(sumsq_ready, c + 1)
                to = (rk_norm, rq_norms[par])[which]
                rsqrt(to[:, :], sumsq[:, which * H:(which + 1) * H]).then_inc(rnorm_ready, 1)

            def layer_norm(which, n):
                pool.wait_ge((var_ready, var2_ready)[which], n)
                rsqrt(rstd[:, which:which + 1], var_eps[:, which:which + 1]).then_inc((rstd_ready, rstd2_ready)[which], 1)

            def add_heads(c, step):
                half, quarter = o_pairs[:, 0:4 * D], o_pairs[:, 4 * D:6 * D]
                if step == 0:
                    pool.wait_ge(o_ready, (c + 1) * G)
                    nc.gpsimd.tensor_tensor(half, o_sb[:, 0:4 * D], o_sb[:, 4 * D:8 * D], ALU.add).then_inc(pool_step, 1)
                elif step == 1:
                    pool.wait_ge(pool_step, 2 * c + 1)
                    nc.gpsimd.tensor_tensor(quarter, half[:, 0:2 * D], half[:, 2 * D:4 * D], ALU.add).then_inc(pool_step, 1)
                else:
                    pool.wait_ge(pool_step, 2 * c + 2)
                    nc.gpsimd.tensor_tensor(y_sb[:, :], quarter[:, 0:D], quarter[:, D:2 * D], ALU.add).then_inc(y_ready, 1)

            def key_update(i, par, l, g):
                pool.wait_ge(level_done, step_done(i, l, g) if l else pair_done(i, 2 * g + 1))
                left = halves(kds[par], g, STEPS[l])[:, :, 0, :]
                nc.gpsimd.tensor_tensor(left, left, spread(block_products(par, g, STEPS[l], 1), STEPS[l]),
                                        ALU.mult).then_inc(kd_ready, 1)

            def offset(numbers):
                return bass.IndirectOffsetOnAxis(ap=numbers, axis=0)

            def route(j):
                pool.wait_ge(slot_ready, j + 1)
                hold(nc.gpsimd.indirect_dma_start(slots_table[:, :].rearrange("r (p one) -> (r p) one", one=1),
                                                  offset(slot_no[:, 0:1]), chunk_rows[:, 0:1],
                                                  None)).then_inc(slots_stored, 16)

            def gather(n, r):
                if not isinstance(n, int) or n >= RING:
                    pool.wait_ge(tile_stored[r], turns(n - RING))
                hold(nc.gpsimd.tensor_copy(token_row[r][:, :], token_rows[:, bass.ds(n, 1)])).then_inc(token_row_ready, 1)
                pool.wait_ge(token_row_ready, n + 1)
                hold(nc.gpsimd.indirect_dma_start(ring[r][:, 0:3 * D], None, rows[:, :],
                                                  offset(token_row[r][:, 0:1]))).then_inc(tile_in[r], 16)

            last_row = pool.to_reg(B * T - 1)

            def tile_step(n, r):
                if live(n):
                    gather(n + AHEAD, (r + AHEAD) % RING)
                if live(n - 2):
                    b = (r - 2) % RING
                    pool.wait_ge(tile_out_ready, n - 1)
                    hold(nc.gpsimd.indirect_dma_start(out[:, :, :].rearrange("b t d -> (b t) d"),
                                                      offset(token_row[b][:, 0:1]), ring[b][:, 3 * D:4 * D], None,
                                                      bounds_check=last_row, oob_is_err=False)).then_inc(tile_stored[b], 16)

            def slot(i, par, parts):
                for what, *n in ORDER:
                    if PART[what] not in parts:
                        continue
                    if what == "route":
                        route(i - 2)
                    elif what == "first" and n[0] % 2:
                        key_update(i, par, 0, n[0] // 2)
                    elif what == "level":
                        if n == [1, 0]:
                            pool.wait_ge(t_ready, i + 1)
                        key_update(i, par, *n)
                    elif what == "rstd1":
                        layer_norm(0, i + 3)
                    elif what == "rnorm":
                        norm(i + 1, 1 - par, *n)
                    elif what == "heads":
                        add_heads(i - 1, *n)
                    elif what == "rstd2":
                        layer_norm(1, i)

            nc.gpsimd.memset(minus_half[:, :], -0.5).then_inc(setup_pool, 1)
            nc.gpsimd.memset(state[:, :], 0.0).then_inc(setup_pool, 1)
            for n in range(2):
                nc.gpsimd.memset(scoress[n][:, :], 0.0).then_inc(setup_pool, 1)
            nc.gpsimd.memset(ones_sb[:, :], 1.0).then_inc(setup_pool, 1)
            pool.wait_ge(setup_pool, 5)
            layer_norm(0, 1)
            pool.wait_ge(table_cleared, 32)
            slots(pool, slot)
            pool.wait_ge(plan_ready, 1)
            pool.wait_ge(slots_stored, 16 * NCHUNK)
            nc.gpsimd.indirect_dma_start(tile_slots[:, :], None, slots_table[:, :],
                                         offset(table_row[0:TILES + AHEAD, 0:1])).then_inc(tile_slots_in, 16)
            pool.wait_ge(token_rows_ready, 1)
            pool.wait_ge(rows_stored, 32 * NCHUNK)
            pool.wait_ge(update_done, NCHUNK * G)
            for n in range(AHEAD):
                gather(n, n)
            tiles(pool, tile_step)
            for n in range(TILES - RING, TILES):
                pool.wait_ge(tile_stored[n % RING], turns(n))
            for n in range(TILES, TILES + AHEAD):
                pool.wait_ge(tile_in[n % RING], turns(n))

        @block.vector
        def _(dve):
            v = nc.vector
            linked = [0]
            base = [0]

            def link(ins):
                ins.then_inc(dve_step, 1)
                linked[0] += 1
                dve.wait_ge(dve_step, base[0] + linked[0])

            def chain_start(i):
                outside = [(n, parts) for n, parts in PROLOGUE + EPILOGUE if n < (i if isinstance(i, int) else 2)]
                steps = in_setup + sum(CHAINED[part] for _, parts in outside for part in parts)
                turns = NCHUNK - 2 if isinstance(i, int) and i >= NCHUNK else 0 if isinstance(i, int) else i - 2
                return turns * sum(CHAINED.values()) + steps

            def layer_norm_var(src, which):
                v.bn_stats(stats[:, which, :], src).then_inc(dve_step, 1)
                linked[0] += 1
                dve.wait_ge(dve_step, base[0] + linked[0])
                link(hold(v.bn_aggr(mean_var[:, which, :], stats[:, which, :])))
                v.tensor_scalar(var_eps[:, which:which + 1], mean_var[:, which, 1:2], LN_EPS, None,
                                ALU.add).then_inc((var_ready, var2_ready)[which], 1)

            def layer_norm_scale(to, src, which, ready):
                v.tensor_scalar(to, src, mean_var[:, which, 0:1], rstd[:, which:which + 1],
                                ALU.subtract, ALU.mult).then_inc(ready, 1)

            def modulate(to, i, scale, shift, ready):
                b = i % B
                v.tensor_scalar(to, bank_m[:, 0:P], mod_t[:, scale, bass.ds(b, 1)], mod_t[:, shift, bass.ds(b, 1)],
                                ALU.mult, ALU.add).then_inc(ready, 1)

            def first_queries(c, par, g):
                dve.wait_ge(q_raw_ready, c * G + g + 1)
                dve.wait_ge(alpha_ready, c * G + g + 1)
                hs = slice(g * HG, (g + 1) * HG)
                q = q_first[:, hs, 0:P].rearrange("p h (n two) -> p h n two", two=2)
                a = alphas[par][:, cols(g)].rearrange("p (h n two) -> p h n two", h=HG, two=2)
                to = qds[par][:, cols(g)].rearrange("p (h n two) -> p h n two", h=HG, two=2)
                odd = q_first[:, hs, P:P + P // 2]
                v.tensor_tensor(odd, q[:, :, :, 1], a[:, :, :, 1], ALU.mult).then_inc(q_first_ready, 1)
                v.tensor_tensor(to[:, :, :, 0], q[:, :, :, 0], a[:, :, :, 0], ALU.mult)
                dve.wait_ge(q_first_ready, q_first_signal(c, 0, g))
                v.tensor_tensor(to[:, :, :, 1], odd, a[:, :, :, 0], ALU.mult).then_inc(q_first_ready, 1)

            def query_update(par, g, l):
                m = STEPS[l]
                right = halves(qds[par], g, m)[:, :, 1, :]
                v.tensor_tensor(right, right, spread(block_products(par, g, m, 0), m), ALU.mult).then_inc(qd_ready, 1)

            def take_norms(c):
                dve.wait_ge(norms_done, 2 * G * (c + 1))
                if not isinstance(c, int) or c:
                    dve.wait_ge(rnorm_ready, 2 * c)
                v.tensor_scalar(sumsq[:, :], bank_m[:, :].rearrange("p (h n) -> p h n", n=SUM_COLS)[:, :, 0], NORM_EPS ** 2, None,
                                ALU.max).then_inc(sumsq_ready, 1)

            def decay_products(c, par, part):
                if part == 0:
                    dve.wait_ge(alpha_ready, (c + 1) * G)
                    if not isinstance(c, int) or c >= 2:
                        dve.wait_ge(state_ready, (c - 1) * G)
                src, n = alphas[par][:, :], H * P
                for m in T_AT:
                    n //= 2
                    if (m > 4) != part:
                        src = t_prods[par][:, T_AT[m]:T_AT[m] + n]
                        continue
                    pair = src.rearrange("p (n two) -> p n two", two=2)
                    dst = t_prods[par][:, T_AT[m]:T_AT[m] + n]
                    ins = v.tensor_tensor(dst, pair[:, :, 0], pair[:, :, 1], ALU.mult)
                    if m == P:
                        ins.then_inc(t_ready, 1)
                    else:
                        link(ins)
                    src = dst

            def take_pair(i, par, pair):
                dve.wait_ge(level_done, pair_done(i, pair))
                by = "p (h t) -> p h t"
                src = bank_l[pair % 2][:, 0:2 * (P + P // 2)].rearrange(by, h=2)
                to = scoress[par][:, pair * 2 * P:(pair + 1) * 2 * P]
                hold(v.copy_predicated(to.rearrange(by, h=2), diag_sb[:, :].rearrange(by, h=2),
                                       src[:, :, 0:P])).then_inc(scores_ready, 1)
                dve.wait_ge(scores_ready, i * NEAR_READS + 2 * pair + 1)
                hold(v.copy_predicated(to.rearrange("p (h n two) -> p h n two", h=2, two=2)[:, :, :, 1],
                                       masks_sb[:, 0, 0:P].rearrange(by, h=2),
                                       src[:, :, P:P + P // 2])).then_inc(scores_ready, 1)

            def take_level(i, par, l, g):
                dve.wait_ge(level_done, step_done(i, l, g))
                query_update(par, g, l)
                if l < NEAR:
                    m = STEPS[l]
                    by = "p (n m) -> p n m"
                    hold(v.copy_predicated(halves(scoress[par], g, m)[:, :, 1, :],
                                           masks_sb[:, l, :].rearrange(by, m=m),
                                           bank_l[g][:, 0:W // 2].rearrange(by, m=m))).then_inc(scores_ready, 1)

            def take_outputs(c, par, g):
                dve.wait_ge(o_done, c * G + g + 1)
                dve.wait_ge(rnorm_ready, 2 * c + 2)
                if g == 0 and (not isinstance(c, int) or c):
                    dve.wait_ge(y_ready, c)
                by = "p (h d) -> p h d"
                v.tensor_tensor(o_sb[:, cols(g)].rearrange(by, h=HG), bank_tail[g][:, :].rearrange(by, h=HG),
                                spread(rq_norms[par][:, g * HG:(g + 1) * HG], P), ALU.mult).then_inc(o_ready, 1)

            def update_state(c, par, g):
                dve.wait_ge(update_done, c * G + g + 1)
                for h in range(g * HG, (g + 1) * HG):
                    s = state[:, bass.ds((c % B) * (H * P) + h * P, P)]
                    at = (h - g * HG) * P
                    last = v.scalar_tensor_tensor(s, s, t_prods[par][:, T_AT[P] + h:T_AT[P] + h + 1],
                                                  bank_tail[g][:, at:at + P], ALU.mult, ALU.add)
                last.then_inc(state_ready, 1)

            def residual(c, par):
                x1 = h2_x1s[par][:, 1, :]
                dve.wait_ge(y_ready, c + 1)
                link(v.tensor_tensor(y_gated[:, :].unsqueeze(1), y_sb[:, :].unsqueeze(1),
                                     mod_rows[:, 0, bass.ds(c % B, 1), :], ALU.mult))
                if not isinstance(c, int) or c >= 2:
                    dve.wait_ge(rows_stored, 32 * (c - 1))
                dve.wait_ge(x_res_in, 16 * (c + 1))
                v.tensor_tensor(x1, y_gated[:, :], x_res[:, :], ALU.add).then_inc(x1_ready, 1)
                dve.wait_ge(x1_ready, c + 1)
                layer_norm_var(x1, 1)

            def norm2(c, par):
                def row(n):
                    return mod_rows[:, n, bass.ds(c % B, 1), :].rearrange("p a d -> p (a d)")

                dve.wait_ge(rstd2_ready, c + 1)
                link(v.scalar_tensor_tensor(scaled2[:, :], h2_x1s[par][:, 1, :], mean_var[:, 1, 0:1], row(2),
                                            ALU.subtract, ALU.mult))
                v.scalar_tensor_tensor(h2_x1s[par][:, 0, :], scaled2[:, :], rstd[:, 1:2], row(3),
                                       ALU.mult, ALU.add).then_inc(h2_ready, 1)

            def choose(j):
                dve.wait_ge(gate_done, j + 1)
                link(v.tensor_tensor(gate_s[:, :], bank_m[:, 256:256 + E], gate_b_sb[:, :], ALU.add))
                link(v.tensor_reduce(gate_max[:, :], gate_s[:, :], AX, ALU.max))
                link(v.scalar_tensor_tensor(gate_rank[:, :], gate_s[:, :], gate_max[:, 0:1], desc_sb[:, :],
                                            ALU.is_equal, ALU.mult))
                link(v.tensor_reduce(gate_first[:, :], gate_rank[:, :], AX, ALU.max))
                ins = v.tensor_scalar(onehot[:, :], gate_rank[:, :], gate_first[:, 0:1], None, ALU.is_equal)
                ins.then_inc(onehot_ready, 1)

            def route(j):
                dve.wait_ge(ranks_done, j + 1)
                link(v.tensor_tensor(free_by_expert[:, :], bank_m[:, 0:E], next_free[:, :], ALU.add))
                v.tensor_tensor(next_free[:, :], bank_m[:, E:2 * E], next_free[:, :], ALU.add).then_inc(ranks_taken, 1)
                link(v.tensor_tensor(own_slot[:, :], free_by_expert[:, :], onehot[:, :], ALU.mult))
                if not isinstance(j, int) or j:
                    dve.wait_ge(slots_stored, 16 * j)
                v.tensor_copy(chunk_rows[:, :], row_numbers_sb[:, bass.ds(j, 1)])
                link(v.tensor_reduce(slot_number[:, :], own_slot[:, :], AX, ALU.add))
                v.tensor_copy(slot_no[:, :], slot_number[:, :]).then_inc(slot_ready, 1)

            def plan():
                dve.wait_ge(ranks_taken, NCHUNK)
                link(v.tensor_tensor(counts[:, :], next_free[:, :], region_sb[:, :], ALU.subtract))
                link(v.tensor_tensor(started[:, :, :], spread(counts[:, :], NCHUNK),
                                     thresholds_sb[:, :].unsqueeze(1).broadcast_to((P, E, NCHUNK)), ALU.is_gt))
                link(v.tensor_reduce(expert_tiles[:, :], started[:, :, :], AX, ALU.add))
                link(v.tensor_tensor(tiles_earlier[:, :, :], earlier_sb[:, :, :],
                                     expert_tiles[:, :].unsqueeze(1).broadcast_to((P, E, E)), ALU.mult))
                link(v.tensor_reduce(tiles_to[:, :], tiles_earlier[:, :, :], AX, ALU.add))
                link(v.tensor_scalar(passed[:, :], tiles_to[:, 0:E - 1], tile_no_sb[:, 0:1], None, ALU.is_le))
                link(v.tensor_reduce(tile_expert[:, :], passed[:, :], AX, ALU.add))
                link(v.tensor_tensor(tiles_passed[:, :], passed[:, :], expert_tiles[:, 0:E - 1], ALU.mult))
                link(v.tensor_reduce(first_tile[:, :], tiles_passed[:, :], AX, ALU.add))
                link(v.tensor_tensor(tile_within[:, :], tile_no_sb[:, :], first_tile[:, :], ALU.subtract))
                v.scalar_tensor_tensor(table_row[:, :], tile_expert[:, :], float(SLOT_ROWS), tile_within[:, :],
                                       ALU.mult, ALU.add).then_inc(plan_ready, 1)
                dve.wait_ge(plan_done, 1)
                v.tensor_copy(expert_row[:, :], bank_m[0:1, 0:P]).then_inc(expert_row_ready, 1)
                dve.wait_ge(plan_done, 2)
                v.tensor_copy(token_rows[:, :], bank_m[:, 0:TILES + AHEAD]).then_inc(token_rows_ready, 1)

            def tile_step(n, r):
                if live(n):
                    dve.wait_ge(tile_t_done, n + 1)
                    if third(n):
                        dve.wait_ge(tile_hid_done, n - 1)
                    v.tensor_copy(tile_h[r % 2][:, :], bank_t[r % 2][:, 0:P]).then_inc(tile_h_ready, 1)
                if live(n - 2):
                    row = ring[(r - 2) % RING]
                    dve.wait_ge(tile_y_done, n - 1)
                    if third(n - 2):
                        dve.wait_ge(tile_out_ready, n - 3)
                    v.tensor_tensor(gated[r % 2][:, :], bank_out[r % 2][:, 0:D], row[:, 2 * D:3 * D],
                                    ALU.mult).then_inc(gated_ready, 1)
                    dve.wait_ge(gated_ready, n - 1)
                    v.tensor_tensor(row[:, 3 * D:4 * D], gated[r % 2][:, :], row[:, D:2 * D],
                                    ALU.add).then_inc(tile_out_ready, 1)

            def slot(i, par, parts):
                base[0], linked[0] = chain_start(i), 0
                other = 1 - par
                for what, *n in ORDER:
                    if PART[what] not in parts:
                        continue
                    if what == "first":
                        take_pair(i, par, *n)
                    elif what == "level":
                        take_level(i, par, *n)
                    elif what == "norm1":
                        dve.wait_ge(x_next_in, 16 * (i + 3))
                        layer_norm_var(x_next[:, :], 0)
                    elif what == "decays":
                        decay_products(i + 1, other, *n)
                    elif what == "q":
                        first_queries(i + 1, other, *n)
                    elif what == "sumsq":
                        take_norms(i + 1)
                    elif what == "scale1":
                        dve.wait_ge(rstd_ready, i + 3)
                        layer_norm_scale(xn[:, :], x_next[:, :], 0, xn_ready)
                    elif what == "channels":
                        dve.wait_ge(xn_t_done, i + 3)
                        modulate(h_ts[par][:, :], i + 2, CA, SA, h_t_ready)
                    elif what == "outputs":
                        take_outputs(i - 1, other, *n)
                    elif what == "updates":
                        update_state(i - 1, other, *n)
                    elif what == "channels2":
                        dve.wait_ge(h2_t_done, i)
                        v.tensor_copy(h2_t[:, :], bank_m[:, 0:P]).then_inc(h2_t_ready, 1)
                    elif what == "gate":
                        choose(i - 2)
                    elif what == "route":
                        route(i - 2)
                    elif what == "residual":
                        residual(i - 1, other)
                    elif what == "norm2":
                        norm2(i - 1, other)
                assert linked[0] == sum(CHAINED[part] for part in parts)

            dve.wait_ge(weights_in, 16 * NW)
            dve.wait_ge(setup_act, 1)
            v.tensor_tensor(silu_c[:, :], silu_c[:, :], c_sb[:, :], ALU.mult).then_inc(setup_dve, 1)
            dve.wait_ge(setup_pe, 1)
            v.tensor_copy(c_t[:, :], bank_m[:, 0:B]).then_inc(setup_dve, 1)
            dve.wait_ge(setup_dve, 2)
            v.tensor_copy(c_wide[:, :, :], spread(c_t[:, :], P)).then_inc(setup_dve, 1)
            dve.wait_ge(setup_pe, 2)
            v.tensor_copy(mod_t[:, :, :].rearrange("p a b -> p (a b)"), bank_m[:, 64:64 + 6 * B]).then_inc(setup_dve, 1)
            dve.wait_ge(setup_dve, 4)
            v.tensor_scalar(mod_t[:, CA, :], mod_t[:, CA, :], 1.0, None, ALU.add).then_inc(setup_dve, 1)
            dve.wait_ge(setup_pe, 10)
            for n in range(2):
                for half in range(2):
                    src = (bank_a, bank_k, bank_q, bank_h)[2 * n + half][:, :].rearrange("p (b d) -> p b d", d=D)
                    sign = sign_sb[:, :].rearrange("p (b d) -> p b d", d=D)
                    if 2 * n + half:
                        dve.wait_ge(setup_dve, 5 + 2 * n + half)
                    at = slice(half * (B // 2), (half + 1) * (B // 2))
                    g = mod_rows[:, n, at, :]
                    link(v.tensor_scalar(sign, src, 0.0, 2.0, ALU.is_ge, ALU.mult))
                    link(v.scalar_tensor_tensor(g, sign, 1.0, src, ALU.subtract, ALU.mult))
                    link(v.tensor_scalar(g, g, GATE_FLOOR, None, ALU.max))
                    v.scalar_tensor_tensor(g, sign, 1.0, g, ALU.subtract, ALU.mult).then_inc(setup_dve, 1)
            for half in range(2):
                at = slice(half * (B // 2), (half + 1) * (B // 2))
                one_cb, shift = (buf[:, :].rearrange("p (b d) -> p b d", d=D) for buf in (bank_l[half], (bank_y, bank_m)[half]))
                v.tensor_scalar(mod_rows[:, 2, at, :], one_cb, 1.0, None, ALU.add).then_inc(setup_dve, 1)
                v.tensor_copy(mod_rows[:, 3, at, :], shift).then_inc(setup_dve, 1)
            dve.wait_ge(x_next_in, 16)
            layer_norm_var(x_next[:, :], 0)
            dve.wait_ge(rstd_ready, 1)
            dve.wait_ge(setup_dve, 13)
            v.tensor_copy(next_free[:, :], region_sb[:, :]).then_inc(setup_dve, 1)
            dve.wait_ge(wv_t_done, 1)
            v.tensor_copy(o_sb[:, cols(0)], bank_a[:, :])
            v.tensor_copy(o_sb[:, cols(1)], bank_k[:, :]).then_inc(setup_dve, 1)
            dve.wait_ge(setup_pe, 11)
            v.tensor_copy(wvo_sb[:, cols(0)], bank_q[:, :])
            v.tensor_copy(wvo_sb[:, cols(1)], bank_h[:, :]).then_inc(setup_dve, 1)
            layer_norm_scale(xn[:, :], x_next[:, :], 0, xn_ready)
            dve.wait_ge(xn_t_done, 1)
            modulate(h_ts[0][:, :], 0, CA, SA, h_t_ready)
            dve.wait_ge(setup_pool, 5)

            in_setup = linked[0]
            slots(dve, slot)
            base[0], linked[0] = chain_start(NCHUNK + 2), 0
            plan()
            tiles(dve, tile_step)


def kernel(**inputs):
    import numpy as np
    import concourse.bacc as bacc
    from concourse.bass_utils import run_bass_kernel_spmd

    a = {k: np.asarray(v) for k, v in inputs.items()}
    s = np.arange(P)[:, None]
    masks = []
    for m in STEPS[:NEAR]:
        t = np.array([t for t in range(P) if (t // m) % 2])[None, :]
        masks.append(np.tile((s // (2 * m) == t // (2 * m)) & ((s // m) % 2 == 0), (1, HG)))
    arrays = {
        "x": a["L0_attn_x"],
        "wq": a["L0_attn_Wq"], "wk": a["L0_attn_Wk"], "wv": a["L0_attn_Wv"], "wg": a["L0_attn_Wg"],
        "wo": a["L0_attn_Wo"].reshape(H, P, D).transpose(1, 0, 2).reshape(P, H * D),
        "gate_w": a["L0_ffn_Wg"],
        "gate_b": np.broadcast_to(a["L0_ffn_bg"], (P, E)),
        "w1": np.concatenate([a["L0_ffn_W1"], a["L0_ffn_b1"].reshape(E, FC, P).transpose(0, 2, 1)],
                             axis=2).transpose(1, 0, 2).reshape(P, E * EXPERT_W),
        "w2": a["L0_ffn_W2"].reshape(E, FC, P, D).transpose(2, 0, 1, 3).reshape(P, E * FC * D),
        "b2": a["L0_ffn_b2"].reshape(1, E * D),
        "c": a["L0_c"], "wmod": a["L0_wmod"],
        "ident": np.eye(P, dtype=np.float32),
        "level_masks": np.concatenate(masks, axis=1).astype(np.int32),
        "diag_mask": np.tile(np.eye(P, dtype=np.int32), (1, 2)),
        "descending": np.broadcast_to(np.arange(E, 0, -1, dtype=np.float32), (P, E)),
        "before": np.triu(np.ones((P, P), np.float32), 1),
        "earlier": np.broadcast_to(np.tril(np.ones((E, E), np.float32)).reshape(1, E * E), (P, E * E)),
        "thresholds": np.broadcast_to(np.arange(NCHUNK, dtype=np.float32) * P, (P, NCHUNK)),
        "region": np.broadcast_to(np.arange(E, dtype=np.float32) * (SLOT_ROWS * P), (P, E)),
        "tile_no": np.arange(P, dtype=np.float32)[:, None],
        "row_numbers": np.stack([i % B * T + i // B * P + np.arange(P) for i in range(NCHUNK)], 1).astype(np.float32),
        "spare_numbers": (B * T + np.arange(P * TABLE_ROWS) % P).reshape(P, TABLE_ROWS).astype(np.float32),
    }
    nc = bacc.Bacc("TRN2", target_bir_lowering=False, num_devices=1)
    arrays = {k: np.ascontiguousarray(v) for k, v in arrays.items()}
    args = [nc.dram_tensor(k, v.shape, mybir.dt.from_np(v.dtype), kind="ExternalInput").ap()
            for k, v in arrays.items()]
    out = nc.dram_tensor("out", (B, T, D), F32, kind="ExternalOutput").ap()
    rows = nc.dram_tensor("rows", (B * T + P, 3 * D), F32).ap()
    slots_table = nc.dram_tensor("slots_table", (TABLE_ROWS, P), F32).ap()
    adaln_gla_moe(nc, *args, rows, slots_table, out)
    r = run_bass_kernel_spmd(nc, [arrays], core_ids=[0])
    return r.results[0]["out"]
```
